# Optimizing a Trainium2 kernel written in Bass

```python
import numpy as np
import jax
import jax.numpy as jnp

def _softmax(x, axis=-1):
    return jax.nn.softmax(x, axis=axis)

def _gelu(x):
    return jax.nn.gelu(x, approximate=True)

def _silu(x):
    return jax.nn.silu(x)

def _sigmoid(x):
    return jax.nn.sigmoid(x)

def _layernorm(x, axis=-1, eps=1e-05):
    m = jnp.mean(x, axis=axis, keepdims=True)
    v = jnp.var(x, axis=axis, keepdims=True)
    return (x - m) / jnp.sqrt(v + eps)

def _scatter_add(tgt, idx, src, axis=0):
    return tgt.at[idx].add(src)

def _segment_sum(src, seg, n):
    return jax.ops.segment_sum(src, seg, n)
kernel_name = 'mk_seq_preln_d1_jaxref_r4_e8a406'

def setup_inputs(seed: int=0):
    np.random.seed(seed)
    _w = jnp.asarray

    def _L0_attn_setup():
        import jax, jax.numpy as jnp
        import numpy as np
        EPS = 1e-10

        def scores_dtype(x):
            return x.dtype
        key = jax.random.key(seed)
        ks = jax.random.split(key, 5)
        B, S, D, N, H = (2, 512, 256, 16, 64)
        init_range = 0.02
        residual = jax.random.normal(ks[0], (B, S, D), dtype=jnp.float32)
        W_key = jax.random.normal(ks[1], (N, D, H), dtype=jnp.float32) * init_range
        W_query = jax.random.normal(ks[2], (N, D, H), dtype=jnp.float32) * init_range
        W_values = jax.random.normal(ks[3], (N, D, H), dtype=jnp.float32) * init_range
        W_output = jax.random.normal(ks[4], (N, H, D), dtype=jnp.float32) * init_range
        return {'residual': residual, 'W_key': W_key, 'W_query': W_query, 'W_values': W_values, 'W_output': W_output, 'Bias_key': jnp.zeros((N, H), jnp.float32), 'Bias_query': jnp.zeros((N, H), jnp.float32), 'Bias_values': jnp.zeros((N, H), jnp.float32), 'Bias_output': jnp.zeros((D,), jnp.float32)}
    _L0_attn_in = _L0_attn_setup()

    def _L0_ffn_setup():
        import jax, jax.numpy as jnp
        import numpy as np
        GROUP = 16
        EPS = 1e-05

        def _dequant(q, scale):
            w = q.astype(jnp.float32) / 7.5 - 1.0
            return w * jnp.repeat(scale, GROUP, axis=1)

        def _qlora_linear(x, q, scale, bias, la, lb):
            w = _dequant(q, scale)
            base = jnp.einsum('btd,od->bto', x, w) + bias
            lora = jnp.einsum('btr,or->bto', jnp.einsum('btd,rd->btr', x, la), lb)
            return base + lora

        def _layernorm(x, g, b):
            mu = jnp.mean(x, axis=-1, keepdims=True)
            var = jnp.mean(jnp.square(x - mu), axis=-1, keepdims=True)
            return (x - mu) * jax.lax.rsqrt(var + EPS) * g + b
        key = jax.random.key(seed)
        ks = jax.random.split(key, 6)
        D, R, B, T = (256, 32, 8, 1024)
        x = jax.random.normal(ks[0], (B, T, D), dtype=jnp.float32)
        qweights = jax.random.randint(ks[1], (6, D, D), 0, 16, dtype=jnp.int32)
        scales = jax.random.uniform(ks[2], (6, D, D // GROUP), dtype=jnp.float32)
        biases = jax.random.normal(ks[3], (6, D), dtype=jnp.float32) * 0.02
        lora_a = jax.random.normal(ks[4], (6, R, D), dtype=jnp.float32) * 0.02
        lora_b = jax.random.normal(ks[5], (6, D, R), dtype=jnp.float32) * 0.02
        ln_gamma = jnp.ones((3, D), dtype=jnp.float32)
        ln_beta = jnp.zeros((3, D), dtype=jnp.float32)
        return {'x': x, 'qweights': qweights, 'scales': scales, 'biases': biases, 'lora_a': lora_a, 'lora_b': lora_b, 'ln_gamma': ln_gamma, 'ln_beta': ln_beta}
    _L0_ffn_in = _L0_ffn_setup()
    _d = {'L0_attn_residual': _L0_attn_in['residual'], 'L0_attn_W_key': _L0_attn_in['W_key'], 'L0_attn_W_query': _L0_attn_in['W_query'], 'L0_attn_W_values': _L0_attn_in['W_values'], 'L0_attn_W_output': _L0_attn_in['W_output'], 'L0_attn_Bias_key': _L0_attn_in['Bias_key'], 'L0_attn_Bias_query': _L0_attn_in['Bias_query'], 'L0_attn_Bias_values': _L0_attn_in['Bias_values'], 'L0_attn_Bias_output': _L0_attn_in['Bias_output'], 'L0_ffn_qweights': _L0_ffn_in['qweights'], 'L0_ffn_scales': _L0_ffn_in['scales'], 'L0_ffn_biases': _L0_ffn_in['biases'], 'L0_ffn_lora_a': _L0_ffn_in['lora_a'], 'L0_ffn_lora_b': _L0_ffn_in['lora_b'], 'L0_ffn_ln_gamma': _L0_ffn_in['ln_gamma'], 'L0_ffn_ln_beta': _L0_ffn_in['ln_beta']}
    _x0 = _d['L0_attn_residual']
    _d['L0_attn_residual'] = jax.random.normal(jax.random.fold_in(jax.random.key(seed), 1), (2, 2048, 256), dtype=_x0.dtype)
    del _x0
    return _d

def reference(L0_attn_residual, L0_attn_W_key, L0_attn_W_query, L0_attn_W_values, L0_attn_W_output, L0_attn_Bias_key, L0_attn_Bias_query, L0_attn_Bias_values, L0_attn_Bias_output, L0_ffn_qweights, L0_ffn_scales, L0_ffn_biases, L0_ffn_lora_a, L0_ffn_lora_b, L0_ffn_ln_gamma, L0_ffn_ln_beta):

    def _L0_attn_ref(residual, W_key, W_query, W_values, W_output, Bias_key, Bias_query, Bias_values, Bias_output):
        import jax, jax.numpy as jnp
        import numpy as np
        EPS = 1e-10

        def scores_dtype(x):
            return x.dtype
        B, S, D = residual.shape
        N, _, H = W_key.shape
        keys = jnp.einsum('bse,neh->bsnh', residual, W_key) + Bias_key
        queries = jnp.einsum('bse,neh->bsnh', residual, W_query) + Bias_query
        values = jnp.einsum('bse,neh->bsnh', residual, W_values) + Bias_values
        scores = jnp.einsum('bknh,bqnh->bnqk', keys, queries) / jnp.sqrt(jnp.asarray(H, scores_dtype(residual)))
        q_idx = jnp.arange(S)[:, None]
        k_idx = jnp.arange(S)[None, :]
        causal_mask = q_idx < k_idx
        scores = jnp.where(causal_mask[None, None, :, :], jnp.asarray(EPS, scores.dtype), scores)
        probs = jax.nn.softmax(scores, axis=3)
        weighted = jnp.einsum('bnqk,bknh->bqnh', probs, values)
        out = jnp.einsum('bqnh,nhe->bqe', weighted, W_output) + Bias_output
        return out

    def _L0_ffn_ref(x, qweights, scales, biases, lora_a, lora_b, ln_gamma, ln_beta):
        import jax, jax.numpy as jnp
        import numpy as np
        GROUP = 16
        EPS = 1e-05

        def _dequant(q, scale):
            w = q.astype(jnp.float32) / 7.5 - 1.0
            return w * jnp.repeat(scale, GROUP, axis=1)

        def _qlora_linear(x, q, scale, bias, la, lb):
            w = _dequant(q, scale)
            base = jnp.einsum('btd,od->bto', x, w) + bias
            lora = jnp.einsum('btr,or->bto', jnp.einsum('btd,rd->btr', x, la), lb)
            return base + lora

        def _layernorm(x, g, b):
            mu = jnp.mean(x, axis=-1, keepdims=True)
            var = jnp.mean(jnp.square(x - mu), axis=-1, keepdims=True)
            return (x - mu) * jax.lax.rsqrt(var + EPS) * g + b
        h = x
        for blk in range(3):
            i0, i1 = (2 * blk, 2 * blk + 1)
            y = _qlora_linear(h, qweights[i0], scales[i0], biases[i0], lora_a[i0], lora_b[i0])
            y = _layernorm(y, ln_gamma[blk], ln_beta[blk])
            y = jax.nn.gelu(y, approximate=False)
            y = _qlora_linear(y, qweights[i1], scales[i1], biases[i1], lora_a[i1], lora_b[i1])
            h = y + h
        return h
    x = L0_attn_residual
    x = x + _L0_attn_ref(_layernorm(x, axis=-1), L0_attn_W_key, L0_attn_W_query, L0_attn_W_values, L0_attn_W_output, L0_attn_Bias_key, L0_attn_Bias_query, L0_attn_Bias_values, L0_attn_Bias_output)
    x = x + _L0_ffn_ref(_layernorm(x, axis=-1), L0_ffn_qweights, L0_ffn_scales, L0_ffn_biases, L0_ffn_lora_a, L0_ffn_lora_b, L0_ffn_ln_gamma, L0_ffn_ln_beta)
    return x

_drawn_inputs = setup_inputs


def setup_inputs(seed=0):
    import zlib

    import numpy as np

    out = dict(_drawn_inputs(seed))
    spreads = {'L0_attn_Bias_key': (0.0, 2.0),
     'L0_attn_Bias_query': (0.0, 0.8),
     'L0_attn_Bias_values': (0.0, 0.1),
     'L0_attn_Bias_output': (0.0, 0.1),
     'L0_ffn_ln_gamma': (1.0, 0.2),
     'L0_ffn_ln_beta': (0.0, 0.1)}
    factors = {'L0_attn_W_key': 8.0,
     'L0_attn_W_query': 8.0,
     'L0_attn_W_values': 8.0,
     'L0_ffn_biases': 7.861,
     'L0_ffn_lora_a': 4.789,
     'L0_ffn_lora_b': 4.694}
    for name, (base, spread) in spreads.items():
        noise = np.random.default_rng([zlib.crc32(name.encode()), seed]).standard_normal(out[name].shape)
        drawn = base * np.exp(spread * noise) if base else spread * noise
        out[name] = jnp.asarray(drawn.astype(out[name].dtype))
    for name, factor in factors.items():
        out[name] = (out[name] * factor).astype(out[name].dtype)
    return out
```

```python
from contextlib import ExitStack

import numpy as np

import concourse.bass as bass
from concourse import mybir

F32 = mybir.dt.float32
F32R = mybir.dt.float32r
BF16 = mybir.dt.bfloat16
I32 = mybir.dt.int32
ALU = mybir.AluOpType
ACT = mybir.ActivationFunctionType
AX = mybir.AxisListType

P = 128
CH = 512
SCORE_SCALE = 0.125
MASKED_RAW = 8e-10
MASKED = 1e-10
NEVER = -1e30
LN_EPS = 1e-5


def layernorm_and_weights(nc, x, qweights, scales, lora_a, lora_b, xnt, wt):
    n_layers, _, D = qweights.shape
    R = lora_a.shape[1]
    n_chunks = x.shape[0]
    halves = D // P
    groups = D // 16
    with ExitStack() as ctx:
        def sb(name, shape, dt=F32):
            return ctx.enter_context(nc.sbuf_tensor(name, shape, dt))

        def sem(name):
            return ctx.enter_context(nc.semaphore(name))

        ident = sb("a_ident", [P, P])
        minus_half = sb("a_minus_half", [P, 4])
        q_in = sb("a_q_in", [P, halves, D], I32)
        sc_in = sb("a_sc_in", [P, halves, groups])
        la_in = sb("a_la_in", [R, D])
        lb_in = sb("a_lb_in", [P, halves, R])
        w_unit = sb("a_w_unit", [P, halves, D])
        w_deq = sb("a_w_deq", [P, halves, D])
        lbt = sb("a_lbt", [R, D])
        w_t = sb("a_w_t", [P, halves, D])
        x_in = sb("a_x_in", [P, 2, 4, D])
        stats = sb("a_stats", [P, 2, 4, 6])
        mv = sb("a_mv", [P, 2, 4, 2])
        wait_here = sb("a_wait_here", [P, 1])
        var_eps = sb("a_var_eps", [P, 2, 4])
        rstd = sb("a_rstd", [P, 2, 4])
        xn = sb("a_xn", [P, 2, 4, D])
        xt = sb("a_xt", [P, 2, halves, CH])
        ps_w = ctx.enter_context(nc.psum_tensor("a_ps_w", [P, halves, CH], F32))
        ps_b = ctx.enter_context(nc.psum_tensor("a_ps_b", [P, CH], F32))
        ps_x = ctx.enter_context(nc.psum_tensor("a_ps_x", [P, 2, halves, CH], F32))

        ident_zero = sem("a_ident_zero")
        ident_ready = sem("a_ident_ready")
        w_loaded = sem("a_w_loaded")
        w_units = sem("a_w_units")
        w_dequant = sem("a_w_dequant")
        lb_turned = sem("a_lb_turned")
        lbt_ready = sem("a_lbt_ready")
        w_summed = sem("a_w_summed")
        wt_ready = sem("a_wt_ready")
        wt_stored = sem("a_wt_stored")
        x_loaded = [sem(f"a_x_loaded{b}") for b in range(2)]
        stats_done = sem("a_stats_done")
        mv_done = sem("a_mv_done")
        var_done = sem("a_var_done")
        rstd_done = sem("a_rstd_done")
        xn_done = sem("a_xn_done")
        x_turned = sem("a_x_turned")
        xt_ready = sem("a_xt_ready")
        xt_stored = [sem(f"a_xt_stored{b}") for b in range(2)]

        with nc.Block() as block:
            @block.sync
            def _(sp):
                for b in range(2):
                    sp.dma_start(x_in[:, b], x[b]).then_inc(x_loaded[b], 16)
                with sp.Fori(0, n_layers) as l:
                    sp.wait_ge(w_summed, l)
                    sp.dma_start(q_in[:, :, :], qweights[l].rearrange("(h p) d -> p h d", p=P)).then_inc(w_loaded, 16)
                    sp.dma_start(sc_in[:, :, :], scales[l].rearrange("(h p) g -> p h g", p=P)).then_inc(w_loaded, 16)
                    sp.dma_start(la_in[:, :], lora_a[l]).then_inc(w_loaded, 16)
                    sp.dma_start(lb_in[:, :, :], lora_b[l].rearrange("(h p) r -> p h r", p=P)).then_inc(w_loaded, 16)
                    sp.wait_ge(wt_ready, l + 1)
                    sp.dma_start(wt[l], w_t[:, :, :]).then_inc(wt_stored, 16)
                with sp.Fori(0, n_chunks // 2) as i:
                    for b in range(2):
                        sp.wait_ge(xt_ready, 2 * i + b + 1)
                        sp.dma_start(xnt[2 * i + b], xt[:, b]).then_inc(xt_stored[b], 16)
                        sp.dma_start(x_in[:, b], x[(2 * i + b + 2) % n_chunks]).then_inc(x_loaded[b], 16)
                sp.wait_ge(wt_stored, 16 * n_layers)
                for b in range(2):
                    sp.wait_ge(xt_stored[b], 16 * (n_chunks // 2))
                    sp.wait_ge(x_loaded[b], 16 * (n_chunks // 2 + 1))

            @block.gpsimd
            def _(pool):
                nc.gpsimd.memset(ident[:, :], 0.0).then_inc(ident_zero, 1)
                nc.gpsimd.memset(minus_half[:, :], -0.5).then_inc(ident_zero, 1)
                pool.wait_ge(ident_zero, 2)
                nc.gpsimd.affine_select(out=ident[:, :], in_=ident[:, :], compare_op=ALU.not_equal, fill=1.0,
                                        base=0, pattern=[[-1, P]], channel_multiplier=1).then_inc(ident_ready, 1)
                with pool.Fori(0, n_chunks // 2) as i:
                    for b in range(2):
                        pool.wait_ge(var_done, 2 * i + b + 1)
                        nc.gpsimd.tensor_tensor(rstd[:, b], var_eps[:, b], minus_half[:, :],
                                                ALU.pow).then_inc(rstd_done, 1)

            @block.vector
            def _(dve):
                with dve.Fori(0, n_layers) as l:
                    dve.wait_ge(w_loaded, 64 * l + 64)
                    nc.vector.tensor_scalar(w_unit[:, :, :], q_in[:, :, :], 1.0 / 7.5, -1.0,
                                            ALU.mult, ALU.add).then_inc(w_units, 1)
                    dve.wait_ge(w_units, l + 1)
                    dve.wait_ge(w_summed, l)
                    for h in range(halves):
                        last = nc.vector.tensor_tensor(
                            w_deq[:, h].rearrange("p (g e) -> p g e", e=16),
                            w_unit[:, h].rearrange("p (g e) -> p g e", e=16),
                            sc_in[:, h].unsqueeze(2).to_broadcast([P, groups, 16]), ALU.mult)
                    last.then_inc(w_dequant, 1)
                with dve.Fori(0, n_chunks // 2) as i:
                    for b in range(2):
                        dve.wait_ge(x_loaded[b], 16 * i + 16)
                        for t in range(4):
                            nc.vector.bn_stats(stats[:, b, t, :], x_in[:, b, t, :]).then_inc(stats_done, 1)
                        dve.wait_ge(stats_done, 8 * i + 4 * b + 4)
                        nc.vector.memset(wait_here[:, :], 0.0)
                        for t in range(4):
                            nc.vector.bn_aggr(mv[:, b, t, :], stats[:, b, t, :]).then_inc(mv_done, 1)
                        dve.wait_ge(mv_done, 8 * i + 4 * b + 4)
                        nc.vector.tensor_scalar(var_eps[:, b], mv[:, b, :, 1], LN_EPS, None,
                                                ALU.add).then_inc(var_done, 1)
                        dve.wait_ge(rstd_done, 2 * i + b + 1)
                        dve.wait_ge(x_turned, 2 * i)
                        for t in range(4):
                            last = nc.vector.tensor_scalar(xn[:, b, t, :], x_in[:, b, t, :], mv[:, b, t, 0:1],
                                                           rstd[:, b, t:t + 1], ALU.subtract, ALU.mult)
                        last.then_inc(xn_done, 1)

            @block.tensor
            def _(pe):
                pe.wait_ge(ident_ready, 1)
                with pe.Fori(0, n_layers) as l:
                    pe.wait_ge(w_loaded, 64 * l + 64)
                    pe.wait_ge(lbt_ready, l)
                    for h in range(halves):
                        mm = pe.matmul(ps_b[0:R, h * P:(h + 1) * P], lb_in[:, h, :], ident[:, :],
                                       start=(h == 0), stop=True, skip_group_check=True)
                    mm.then_inc(lb_turned, 1)
                    pe.wait_ge(w_dequant, l + 1)
                    pe.wait_ge(wt_ready, l)
                    for s in range(halves):
                        for h in range(halves):
                            pe.matmul(ps_w[:, s, h * P:(h + 1) * P], w_deq[:, h, s * P:(s + 1) * P], ident[:, :],
                                      start=(h == 0), stop=False, skip_group_check=True)
                    pe.wait_ge(lbt_ready, l + 1)
                    for s in range(halves):
                        mm = pe.matmul(ps_w[:, s, 0:D], la_in[:, s * P:(s + 1) * P], lbt[:, :],
                                       start=False, stop=True, skip_group_check=True)
                    mm.then_inc(w_summed, 1)
                with pe.Fori(0, n_chunks // 2) as i:
                    for b in range(2):
                        pe.wait_ge(xn_done, 2 * i + b + 1)
                        pe.wait_ge(xt_ready, 2 * i)
                        for s in range(halves):
                            for t in range(4):
                                mm = pe.transpose(ps_x[:, b, s, t * P:(t + 1) * P],
                                                  xn[:, b, t, s * P:(s + 1) * P], ident[:, :])
                        mm.then_inc(x_turned, 1)

            @block.scalar
            def _(act):
                with act.Fori(0, n_layers) as l:
                    act.wait_ge(lb_turned, l + 1)
                    act.wait_ge(w_summed, l)
                    nc.scalar.copy(lbt[:, :], ps_b[0:R, 0:D]).then_inc(lbt_ready, 1)
                    act.wait_ge(w_summed, l + 1)
                    act.wait_ge(wt_stored, 16 * l)
                    nc.scalar.copy(w_t[:, :, :], ps_w[:, :, 0:D]).then_inc(wt_ready, 1)
                with act.Fori(0, n_chunks // 2) as i:
                    for b in range(2):
                        act.wait_ge(x_turned, 2 * i + b + 1)
                        act.wait_ge(xt_stored[b], 16 * i)
                        nc.scalar.copy(xt[:, b], ps_x[:, b]).then_inc(xt_ready, 1)


def tiles_of(group):
    order = [1, 2, 3, 0] if group == 3 else list(range(group + 1))
    out = []
    for chunk in order:
        for half in range(2):
            tile, at = [], 0
            for r in (2 * half, 2 * half + 1):
                q0 = 128 * r if chunk == group else 0
                w = CH - q0
                if at and at + w > CH:
                    at = CH
                tile.append((4 * chunk + r, q0, w, at))
                at += w
            out.append(tile)
    return out


GROUPS = [3, 2, 1, 0]
TILES = [(g, tile) for g in GROUPS for tile in tiles_of(g)]
NT = len(TILES)
FIRST_TILE = {g: min(t for t in range(NT) if TILES[t][0] == g) for g in GROUPS}
LAST_TILE = {g: max(t for t in range(NT) if TILES[t][0] == g) for g in GROUPS}
SLOTS = 6 * NT
NP_SLOTS = 3


def pool_ops_before(t):
    n = 0
    for k in range(min(t, LAST_TILE[1] + 1)):
        n += 2 if k == FIRST_TILE[TILES[k][0]] else 4
    return n


POOL_OPS = pool_ops_before(NT)


def slot_user_before(t):
    if t >= NP_SLOTS:
        return 0, t - NP_SLOTS
    return 1, max(k for k in range(NT) if k % NP_SLOTS == t % NP_SLOTS)


MAX_UNITS = [(h, qb, u, min(CH, 128 * (qb + 1) - CH * u))
             for c in GROUPS for qb in range(4 * c + 3, 4 * c - 1, -1) for u in range(c + 1) for h in range(2)]
NMAX = len(MAX_UNITS)
NPROJ = 12
PROJ_SLOT = [3 * u for u in range(NPROJ)]
MAX_SLOT = 37
LAST_MAX = {c: max(v for v in range(NMAX) if MAX_UNITS[v][1] // 4 == c) for c in GROUPS}

FIN = [("bc", 3, 8), ("vt", 3, 50), ("den", 3, 62), ("bc", 2, 66), ("mt", 3, 72), ("vt", 2, 86),
       ("mt", 2, 96), ("den", 2, 98), ("bc", 1, 101), ("vt", 1, 110), ("mt", 1, 112), ("den", 1, 116),
       ("bc", 0, 118), ("mt", 0, 119), ("den", 0, SLOTS), ("vt", 0, SLOTS)]
NFIN = len(FIN)
FIN_FIRST = [("mt", 3), ("mt", 2), ("mt", 1), ("mt", 0), ("vt", 3), ("vt", 2), ("vt", 1), ("vt", 0)]
NFIRST = len(FIN_FIRST)


def attention(nc, xnt, w_qkv, b_qkv, ot):
    n_chunks, _, halves, _ = xnt.shape
    n_b = n_chunks // 4
    n_pairs = w_qkv[0].shape[0] // 2
    N = n_b * n_pairs
    S = 4 * CH
    with ExitStack() as ctx:
        def sb(name, shape, dt=F32):
            return ctx.enter_context(nc.sbuf_tensor(name, shape, dt))

        def sem(name):
            return ctx.enter_context(nc.semaphore(name))

        ident = sb("ident", [P, P])
        ident_bf = sb("ident_bf", [P, P], BF16)
        never_above = sb("never_above", [P, P], BF16)
        mask_q = sb("mask_q", [P, CH])
        ones64 = sb("ones64", [P, 64])
        ones_row = sb("ones_row", [P, CH], BF16)
        select = sb("select", [P, 2, P], F32R)
        keys_after = sb("keys_after", [P, CH])
        masked_bias = sb("masked_bias", [P, 1])

        w_in = sb("w_in", [P, halves, 3, P])
        bias = sb("bias", [P, 3])
        xs = sb("xs", [P, 2, halves, CH])
        hi = [sb(f"hi_{m}", [P, S], F32R) for m in "qk"]
        lo = [sb(f"lo_{m}", [P, S], F32R) for m in "qk"]
        vt = sb("vt", [P, S])
        q_pad = [sb(f"q_pad{h}", [P, S], BF16) for h in range(2)]
        k_bf = sb("k_bf", [P, S], BF16)
        partial = sb("partial", [P, 2, 16, 5])
        neg_max = sb("neg_max", [P, 4, 8])
        m_row = sb("m_row", [8, 4, P], F32R)
        junk = sb("junk", [P, 2, CH], BF16)
        wait_here = sb("wait_here", [P, 4])

        qq = [sb(f"qq{h}", [P, S], F32R) for h in range(2)]
        qm = [sb(f"qm{h}", [P, S], F32R) for h in range(2)]
        kk = [sb(f"kk{h}", [P, S], F32R) for h in range(2)]
        kl = [sb(f"kl{h}", [P, S], F32R) for h in range(2)]
        v = sb("v", [P, 16, P])
        v_sum = sb("v_sum", [P, S])
        v_tail = sb("v_tail", [P, 5])
        probs = [sb(f"probs{h}", [P, NP_SLOTS, 2 * CH]) for h in range(2)]
        acc = [sb(f"acc{h}", [P, CH]) for h in range(2)]
        e0 = sb("e0", [P, CH])
        masked_num = sb("masked_num", [P, CH])
        masked_den = sb("masked_den", [P, CH])
        num = sb("num", [P, CH])
        rden = sb("rden", [P, CH])
        o_out = sb("o_out", [P, 2, CH])

        ps_s = ctx.enter_context(nc.psum_tensor("ps_s", [P, 2, 2 * CH], F32))
        ps_bg = ctx.enter_context(nc.psum_tensor("ps_bg", [P, 2, CH], F32))
        ps_o = ctx.enter_context(nc.psum_tensor("ps_o", [P, CH], F32))
        ps_fin = ctx.enter_context(nc.psum_tensor("ps_fin", [P, CH], F32))

        zeroed = sem("zeroed")
        shaped = sem("shaped")
        set_up = sem("set_up")
        consts = sem("consts")
        counted = sem("counted")
        w_loaded = sem("w_loaded")
        xs_loaded = [sem(f"xs_loaded{b}") for b in range(2)]
        proj_done = sem("proj_done")
        hi_ready = sem("hi_ready")
        proj_read = sem("proj_read")
        bf_ready = sem("bf_ready")
        max_scores = sem("max_scores")
        max_read = sem("max_read")
        max_ready = sem("max_ready")
        stack_in = [sem(f"stack_in{c}") for c in range(4)]
        row_in = [sem(f"row_in{c}") for c in range(4)]
        fin_written = sem("fin_written")
        fin_read = sem("fin_read")
        s_ready = sem("s_ready")
        p_ready = sem("p_ready")
        pv_done = sem("pv_done")
        added = sem("added")
        sums_ready = sem("sums_ready")
        tail_ready = sem("tail_ready")
        e0_ready = sem("e0_ready")
        step = sem("step")
        num_ready = sem("num_ready")
        o_ready = sem("o_ready")
        o_stored = [sem(f"o_stored{b}") for b in range(2)]

        def cols(c):
            return slice(CH * c, CH * (c + 1))

        def fin_before(i, k):
            return NFIN * i + NFIRST + k

        def fin_index(kind, c):
            return [e[:2] for e in FIN].index((kind, c))

        with nc.Block() as block:
            @block.sync
            def _(sp):
                def load_weights(j):
                    sp.wait_ge(proj_read, NPROJ * j)
                    pair = j % n_pairs
                    for m in range(3):
                        for s in range(halves):
                            sp.dma_start(w_in[:, s, m, :].rearrange("p (n h) -> p n h", n=2),
                                         w_qkv[m].rearrange("(a n) (s p) h -> a s p n h", n=2, p=P)[pair, s]
                                         ).then_inc(w_loaded, 16)
                        sp.dma_start(bias[:, m:m + 1],
                                     b_qkv[m].rearrange("(a n) (h o) -> a (n h) o", n=2, o=1)[pair]
                                     ).then_inc(w_loaded, 16)

                def load_x(j, c):
                    sp.wait_ge(proj_done, NPROJ * j + (3 * (c - 1) if c >= 2 else 0))
                    sp.dma_start(xs[:, c % 2], xnt[4 * ((j // n_pairs) % n_b) + c]).then_inc(xs_loaded[c % 2], 16)

                def install(j, c):
                    sp.wait_ge(proj_read, NPROJ * (j + 1))
                    for h in range(2):
                        own = slice(64 * h, 64 * h + 64)
                        for dst, rows, src in ((qq[h], slice(0, 64), hi[0]), (qq[h], slice(64, 128), lo[0]),
                                               (qm[h], slice(0, 64), hi[0]), (kk[h], slice(0, 64), hi[1]),
                                               (kk[h], slice(64, 128), hi[1]), (kl[h], slice(0, 64), lo[1])):
                            sp.dma_start(dst[rows, cols(c)].bitcast(F32), src[own, cols(c)].bitcast(F32)
                                         ).then_inc(stack_in[c], 16)

                def install_max(c, written):
                    sp.wait_ge(fin_read, written)
                    for h in range(2):
                        for r in range(4):
                            at = CH * c + P * r
                            sp.dma_start(qm[h][64:65, at:at + P].bitcast(F32),
                                         m_row[4 * h + r:4 * h + r + 1, c, :].bitcast(F32)).then_inc(row_in[c], 16)

                sp.wait_ge(consts, 1)
                load_weights(0)
                for c in range(4):
                    load_x(0, c)
                for c in GROUPS:
                    install(0, c)
                load_weights(1)
                for c in range(2):
                    load_x(1, c)
                for k, (kind, c) in enumerate(FIN_FIRST):
                    if kind == "mt":
                        install_max(c, k + 1)
                with sp.Fori(0, N) as i:
                    for c in (2, 3):
                        load_x(i + 1, c)
                    load_weights(i + 2)
                    for c in (0, 1):
                        load_x(i + 2, c)
                    for c in GROUPS:
                        sp.wait_ge(pv_done, NT * i + LAST_TILE[c] + 1)
                        install(i + 1, c)
                        install_max(c, fin_before(i, fin_index("mt", c)) + 1)
                        sp.wait_ge(o_ready, 4 * i + (3 - c) + 1)
                        sp.dma_start(ot[i // n_pairs, i % n_pairs, 3 - c], o_out[:, c % 2]).then_inc(o_stored[c % 2], 16)
                for b in range(2):
                    sp.wait_ge(o_stored[b], 16 * 2 * N)
                    sp.wait_ge(xs_loaded[b], 16 * (2 * N + 3))
                for c in range(4):
                    sp.wait_ge(stack_in[c], 192 * (N + 1))
                    sp.wait_ge(row_in[c], 128 * (N + 1))
                sp.wait_ge(w_loaded, 144 * (N + 2))

            @block.gpsimd
            def _(pool):
                g = nc.gpsimd
                for tile in (ident, ident_bf, never_above, mask_q):
                    g.memset(tile[:, :], 0.0).then_inc(zeroed, 1)
                pool.wait_ge(zeroed, 4)
                for tile in (ident, ident_bf):
                    g.affine_select(out=tile[:, :], in_=tile[:, :], compare_op=ALU.not_equal, fill=1.0,
                                    base=0, pattern=[[-1, P]], channel_multiplier=1).then_inc(shaped, 1)
                g.affine_select(out=never_above[:, :], in_=never_above[:, :], compare_op=ALU.is_ge, fill=NEVER,
                                base=0, pattern=[[1, P]], channel_multiplier=-1).then_inc(shaped, 1)
                tri = mask_q[:, CH - P:CH]
                g.affine_select(out=tri, in_=tri, compare_op=ALU.is_ge, fill=NEVER,
                                base=0, pattern=[[-1, P]], channel_multiplier=1).then_inc(shaped, 1)
                pool.wait_ge(counted, 1)
                for h in range(2):
                    col = partial[:, h, 15, 4:5]
                    g.affine_select(out=col, in_=col, compare_op=ALU.not_equal, fill=NEVER,
                                    base=-(P - 1), pattern=[[0, 1]], channel_multiplier=1).then_inc(shaped, 1)
                with pool.Fori(0, N) as i:
                    n = 0
                    for t in range(LAST_TILE[1] + 1):
                        group, tile = TILES[t]
                        pool.wait_ge(p_ready, 2 * NT * i + 2 * t + 2)
                        if t == FIRST_TILE[group]:
                            if group < 3:
                                pool.wait_ge(fin_written, fin_before(i, fin_index("den", group + 1)) + 1)
                            else:
                                pool.wait_ge(fin_written, fin_before(i, 0))
                            for h in range(2):
                                pr = probs[h][:, t % NP_SLOTS]
                                g.tensor_tensor(acc[h][:, :], pr[:, 0:CH], pr[:, CH:2 * CH], ALU.add).then_inc(added, 1)
                            n += 2
                            continue
                        for kb, q0, w, at in tile:
                            for h in range(2):
                                pool.wait_ge(added, POOL_OPS * i + n - 1)
                                g.tensor_tensor(acc[h][:, q0:q0 + w], acc[h][:, q0:q0 + w],
                                                probs[h][:, t % NP_SLOTS, at:at + w], ALU.add).then_inc(added, 1)
                                n += 1

            @block.tensor
            def _(pe):
                def project(j, u):
                    c, m = divmod(u, 3)
                    if u == 0:
                        pe.wait_ge(w_loaded, 144 * (j + 1))
                        pe.wait_ge(max_read, NMAX * j)
                    if m == 0:
                        pe.wait_ge(xs_loaded[c % 2], 16 * (2 * j + c // 2 + 1))
                    if u >= 2:
                        pe.wait_ge(proj_read, NPROJ * j + u - 1)
                    for s in range(halves):
                        mm = pe.matmul(ps_bg[:, u % 2, :], w_in[:, s, m, :], xs[:, c % 2, s, :],
                                       start=(s == 0), stop=(s == halves - 1))
                    mm.then_inc(proj_done, 1)

                def max_unit(j, n):
                    h, qb, u, w = MAX_UNITS[n]
                    if n == 0:
                        pe.wait_ge(bf_ready, 4 * (j + 1))
                    if n < 2:
                        pe.wait_ge(proj_read, NPROJ * (j + 1))
                    else:
                        pe.wait_ge(max_read, NMAX * j + n - 1)
                    pe.matmul(ps_bg[:, n % 2, 0:w], q_pad[h][:, qb * P:(qb + 1) * P], k_bf[:, CH * u:CH * u + w],
                              start=True, stop=True).then_inc(max_scores, 1)

                def turn_max(j, c, before):
                    pe.wait_ge(max_ready, 4 * j + (3 - c) + 1)
                    pe.wait_ge(fin_read, before)
                    pe.matmul(ps_fin[0:8, 0:P], neg_max[:, c, :], ident[:, :],
                              start=True, stop=True).then_inc(fin_written, 1)

                def turn_values(c, before):
                    pe.wait_ge(fin_read, before)
                    for r in range(4):
                        mm = pe.transpose(ps_fin[:, r * P:(r + 1) * P], vt[:, CH * c + r * P:CH * c + (r + 1) * P],
                                          ident[:, :])
                    mm.then_inc(fin_written, 1)

                def spread_max(group, before):
                    pe.wait_ge(fin_read, before)
                    for h in range(2):
                        mm = pe.matmul(ps_fin[:, :], select[:, h, :], qm[h][:, cols(group)],
                                       start=(h == 0), stop=(h == 1))
                    mm.then_inc(fin_written, 1)

                def denominators(i, group, before):
                    pe.wait_ge(fin_read, before)
                    if group:
                        pe.wait_ge(added, POOL_OPS * i + pool_ops_before(LAST_TILE[group] + 1))
                        for h in range(2):
                            mm = pe.matmul(ps_fin[64 * h:64 * h + 64, :], ones64[:, :], acc[h][:, :],
                                           start=True, stop=True, skip_group_check=True)
                    else:
                        for t in range(FIRST_TILE[0], NT):
                            for kb, q0, w, at in TILES[t][1]:
                                for h in range(2):
                                    mm = pe.matmul(ps_fin[64 * h:64 * h + 64, q0:q0 + w], ones64[:, :],
                                                   probs[h][:, t % NP_SLOTS, at:at + w],
                                                   start=(kb == 0), stop=(kb == 3), skip_group_check=True)
                    mm.then_inc(fin_written, 1)

                def scores_wait(i, t, h):
                    group, tile = TILES[t]
                    if h == 0 and t == FIRST_TILE[group]:
                        pe.wait_ge(row_in[group], 128 * (i + 1))
                    if h == 0 and t == 0:
                        for c in (3, 2, 1):
                            pe.wait_ge(stack_in[c], 192 * (i + 1))
                    if h == 0 and t == LAST_TILE[3] - 1:
                        pe.wait_ge(stack_in[0], 192 * (i + 1))

                def scores(t, h, n):
                    group, tile = TILES[t]
                    kb, q0, w, at = tile[n]
                    q = slice(CH * group + q0, CH * (group + 1))
                    diagonal = kb // 4 == group
                    out = ps_s[:, h, at:at + w]
                    pe.matmul(out, kk[h][:, kb * P:(kb + 1) * P], qq[h][:, q], start=True, stop=False,
                              skip_group_check=True)
                    mm = pe.matmul(out, kl[h][:, kb * P:(kb + 1) * P], qm[h][:, q], start=False,
                                   stop=not diagonal, skip_group_check=True)
                    if diagonal:
                        mm = pe.matmul(ps_s[:, h, at:at + P], ident_bf[:, :], never_above[:, :], start=False,
                                       stop=True, skip_group_check=True)
                    if n == 1:
                        mm.then_inc(s_ready, 1)

                def weighted(i, t, n):
                    group, tile = TILES[t]
                    kb, q0, w, at = tile[n]
                    if n == 0:
                        pe.wait_ge(p_ready, 2 * NT * i + 2 * t + 2)
                        if t == FIRST_TILE[group]:
                            pe.wait_ge(num_ready, 4 * i + (3 - group))
                    first = t == FIRST_TILE[group] and n == 0
                    last = t == LAST_TILE[group] and n == 1
                    for h in range(2):
                        mm = pe.matmul(ps_o[64 * h:64 * h + 64, q0:q0 + w], v[:, kb, 64 * h:64 * h + 64],
                                       probs[h][:, t % NP_SLOTS, at:at + w], start=first, stop=last,
                                       skip_group_check=True)
                    if n == 1:
                        mm.then_inc(pv_done, 1)

                def between(i, n):
                    for u in range(NPROJ):
                        if PROJ_SLOT[u] == n:
                            project(i + 1, u)
                    if MAX_SLOT <= n < MAX_SLOT + NMAX:
                        max_unit(i + 1, n - MAX_SLOT)
                    for k, (kind, c, at) in enumerate(FIN):
                        if at != n:
                            continue
                        before = fin_before(i, k)
                        if kind == "bc":
                            spread_max(c, before)
                        elif kind == "vt":
                            turn_values(c, before)
                        elif kind == "den":
                            denominators(i, c, before)
                        else:
                            turn_max(i + 1, c, before)

                pe.wait_ge(consts, 1)
                for u in range(NPROJ):
                    project(0, u)
                for n in range(NMAX):
                    max_unit(0, n)
                for k, (kind, c) in enumerate(FIN_FIRST):
                    if kind == "mt":
                        turn_max(0, c, k)
                    else:
                        turn_values(c, k)
                for h in range(2):
                    scores_wait(0, 0, h)
                    for n in range(2):
                        scores(0, h, n)
                with pe.Fori(0, N) as i:
                    for t in range(NT):
                        ni, nt = (i, t + 1) if t < NT - 1 else (i + 1, 0)
                        for h in range(2):
                            scores_wait(ni, nt, h)
                            pe.wait_ge(p_ready, 2 * NT * i + 2 * t + h + 1)
                            for n in range(2):
                                scores(nt, h, n)
                                between(i, 6 * t + 2 * h + n)
                        for n in range(2):
                            weighted(i, t, n)
                            between(i, 6 * t + 4 + n)
                    between(i, SLOTS)

            @block.scalar
            def _(act):
                def high(j, u):
                    c, m = divmod(u, 3)
                    if m == 2:
                        return
                    act.wait_ge(proj_done, NPROJ * j + u + 1)
                    act.wait_ge(stack_in[c], 192 * j)
                    nc.scalar.activation(hi[m][:, cols(c)], ps_bg[:, u % 2, :], ACT.Identity,
                                         bias=bias[:, m:m + 1]).then_inc(hi_ready, 1)

                def evacuate(j, kind, c, written):
                    act.wait_ge(fin_written, written)
                    if kind == "vt":
                        nc.scalar.copy(v[:, 4 * c:4 * c + 4, :].rearrange("p b h -> p (b h)"), ps_fin[:, :]
                                       ).then_inc(fin_read, 1)
                    elif kind == "mt":
                        act.wait_ge(row_in[c], 128 * j)
                        nc.scalar.copy(m_row[:, c, :], ps_fin[0:8, 0:P]).then_inc(fin_read, 1)

                def masked_weight(i, group, written):
                    act.wait_ge(fin_written, written)
                    act.wait_ge(step, 3 * (4 * i + 3 - group))
                    nc.scalar.activation(e0[:, :], ps_fin[:, :], ACT.Exp, bias=masked_bias[:, 0:1],
                                         scale=SCORE_SCALE).then_inc(fin_read, 1)

                act.wait_ge(w_loaded, 144)
                act.wait_ge(consts, 1)
                for u in range(NPROJ):
                    high(0, u)
                for k, (kind, c) in enumerate(FIN_FIRST):
                    evacuate(0, kind, c, k + 1)
                with act.Fori(0, N) as i:
                    for t in range(NT):
                        group, tile = TILES[t]
                        width = tile[1][3] + tile[1][2]
                        for h in range(2):
                            act.wait_ge(s_ready, 2 * NT * i + 2 * t + h + 1)
                            if h == 0:
                                ago, k = slot_user_before(t)
                                if ago == 0:
                                    act.wait_ge(pv_done, NT * i + k + 1)
                                if ago == 0 and k <= LAST_TILE[1]:
                                    act.wait_ge(added, POOL_OPS * i + pool_ops_before(k + 1))
                                if ago == 1:
                                    act.wait_ge(fin_written, fin_before(i, 0))
                                    act.wait_ge(added, POOL_OPS * i)
                            nc.scalar.activation(probs[h][:, t % NP_SLOTS, 0:width], ps_s[:, h, 0:width], ACT.Exp,
                                                 scale=SCORE_SCALE).then_inc(p_ready, 1)
                        for n in range(6 * t, 6 * t + 6 + (t == NT - 1)):
                            for u in range(NPROJ):
                                if PROJ_SLOT[u] == n:
                                    high(i + 1, u)
                            for k, (kind, c, at) in enumerate(FIN):
                                if at == n:
                                    if kind == "bc":
                                        masked_weight(i, c, fin_before(i, k) + 1)
                                    elif kind != "den":
                                        evacuate(i + 1, kind, c, fin_before(i, k) + 1)

            @block.vector
            def _(dve):
                e = nc.vector

                def low(j, u):
                    c, m = divmod(u, 3)
                    if m == 2:
                        dve.wait_ge(proj_done, NPROJ * j + u + 1)
                        e.tensor_scalar(vt[:, cols(c)], ps_bg[:, u % 2, :], bias[:, 2:3], None,
                                        ALU.add).then_inc(proj_read, 1)
                        return
                    dve.wait_ge(hi_ready, 8 * j + 2 * c + m + 1)
                    e.scalar_tensor_tensor(lo[m][:, cols(c)], ps_bg[:, u % 2, :], bias[:, m:m + 1],
                                           hi[m][:, cols(c)].bitcast(F32), ALU.add, ALU.subtract
                                           ).then_inc(proj_read, 1)
                    if m == 0:
                        for h in range(2):
                            own = slice(64 * h, 64 * h + 64)
                            e.tensor_copy(q_pad[h][own, cols(c)], hi[0][own, cols(c)].bitcast(F32))
                    else:
                        e.tensor_copy(k_bf[:, cols(c)], hi[1][:, cols(c)].bitcast(F32)).then_inc(bf_ready, 1)

                def take_max(j, n):
                    h, qb, u, w = MAX_UNITS[n]
                    dve.wait_ge(max_scores, NMAX * j + n + 1)
                    if u == qb // 4:
                        e.memset(wait_here[:, n % 4:n % 4 + 1], 0.0)
                    to = partial[:, h, qb, u:u + 1]
                    if u == qb // 4:
                        e.tensor_tensor_reduce(junk[:, n % 2, 0:w], ps_bg[:, n % 2, 0:w], mask_q[:, CH - w:CH], 1.0,
                                               3 * NEVER, ALU.add, ALU.max, to).then_inc(max_read, 1)
                    else:
                        e.reduce_max(to, ps_bg[:, n % 2, 0:w], AX.X).then_inc(max_read, 1)
                    c = qb // 4
                    if n == LAST_MAX[c]:
                        dve.wait_ge(max_read, NMAX * j + n + 1)
                        e.tensor_reduce(neg_max[:, c, :].rearrange("p (h r) -> p h r", h=2),
                                        partial[:, :, 4 * c:4 * c + 4, :], AX.X, ALU.max,
                                        negate=True).then_inc(max_ready, 1)

                def scan(j, c):
                    e.tensor_tensor_scan(out=v_sum[:, cols(c)], data0=ones_row[:, :], data1=vt[:, cols(c)],
                                         initial=0.0, op0=ALU.mult, op1=ALU.add).then_inc(sums_ready, 1)
                    dve.wait_ge(sums_ready, 4 * j + (3 - c) + 1)
                    if c < 3:
                        dve.wait_ge(tail_ready, 4 * j + (3 - c))
                    e.tensor_tensor(v_tail[:, c:c + 1], v_tail[:, c + 1:c + 2], v_sum[:, CH * c + CH - 1:CH * c + CH],
                                    ALU.add).then_inc(tail_ready, 1)

                def masked_part(i, group, read):
                    dve.wait_ge(fin_read, read)
                    base = 3 * (4 * i + 3 - group)
                    dve.wait_ge(tail_ready, 4 * (i + 1))
                    e.tensor_scalar(e0[:, :], e0[:, :], 1.0, None, ALU.min).then_inc(step, 1)
                    dve.wait_ge(step, base + 1)
                    e.scalar_tensor_tensor(masked_num[:, :], v_sum[:, cols(group)], v_tail[:, group:group + 1],
                                           e0[:, :], ALU.subtract, ALU.mult).then_inc(step, 1)
                    e.scalar_tensor_tensor(masked_den[:, :], keys_after[:, :], float(CH * (3 - group)),
                                           e0[:, :], ALU.add, ALU.mult).then_inc(step, 1)

                def take_numerator(i, group):
                    dve.wait_ge(pv_done, NT * i + LAST_TILE[group] + 1)
                    dve.wait_ge(step, 3 * (4 * i + 3 - group) + 2)
                    e.tensor_tensor(num[:, :], ps_o[:, :], masked_num[:, :], ALU.subtract).then_inc(num_ready, 1)

                def normalise(i, group, written):
                    n = 4 * i + 3 - group
                    dve.wait_ge(fin_written, written)
                    dve.wait_ge(step, 3 * n + 3)
                    e.tensor_tensor(rden[:, :], ps_fin[:, :], masked_den[:, :], ALU.add).then_inc(fin_read, 1)
                    dve.wait_ge(fin_read, written)
                    e.reciprocal(rden[:, :], rden[:, :]).then_inc(counted, 1)
                    dve.wait_ge(counted, 1 + n + 1)
                    dve.wait_ge(num_ready, n + 1)
                    dve.wait_ge(o_stored[group % 2], 16 * (2 * i + (3 - group) // 2))
                    e.tensor_tensor(o_out[:, group % 2, :], num[:, :], rden[:, :], ALU.mult).then_inc(o_ready, 1)

                e.memset(partial[:, :, :, 0:4], 3 * NEVER)
                e.memset(partial[:, :, :, 4:5], MASKED_RAW)
                e.memset(ones_row[:, :], 1.0).then_inc(counted, 1)
                for h in range(2):
                    e.memset(q_pad[h][:, :], 0.0)
                    e.memset(qm[h][64:128, :].bitcast(F32), 0.0)
                    e.memset(kl[h][64:128, :].bitcast(F32), 0.0)
                    e.memset(select[:, h, :].bitcast(F32), 0.0)
                e.memset(ones64[:, :], 1.0)
                e.memset(v_tail[:, :], 0.0)
                e.memset(masked_bias[:, :], MASKED)
                e.memset(neg_max[:, :, :], 0.0).then_inc(set_up, 1)
                dve.wait_ge(set_up, 1)
                for h in range(2):
                    e.memset(kl[h][64:65, :].bitcast(F32), 1.0)
                    e.memset(select[64:65, h, 64 * h:64 * h + 64].bitcast(F32), 1.0)
                dve.wait_ge(counted, 1)
                e.tensor_tensor_scan(out=num[:, :], data0=ones_row[:, :], data1=ones_row[:, :], initial=0.0,
                                     op0=ALU.mult, op1=ALU.add).then_inc(set_up, 1)
                dve.wait_ge(set_up, 2)
                dve.wait_ge(shaped, 6)
                e.tensor_scalar(keys_after[:, :], num[:, :], -1.0, float(CH), ALU.mult, ALU.add).then_inc(consts, 1)
                dve.wait_ge(consts, 1)

                dve.wait_ge(w_loaded, 144)
                for u in range(NPROJ):
                    low(0, u)
                for n in range(NMAX):
                    take_max(0, n)
                for c in GROUPS:
                    scan(0, c)
                with dve.Fori(0, N) as i:
                    for n in range(SLOTS + 1):
                        for g in (3, 2, 1):
                            if n == 6 * (LAST_TILE[g] + 1):
                                take_numerator(i, g)
                        for u in range(NPROJ):
                            if PROJ_SLOT[u] == n:
                                low(i + 1, u)
                        if MAX_SLOT <= n < MAX_SLOT + NMAX:
                            take_max(i + 1, n - MAX_SLOT)
                        for k, (kind, c, at) in enumerate(FIN):
                            if at == n:
                                if kind == "bc":
                                    masked_part(i, c, fin_before(i, k) + 1)
                                elif kind == "den":
                                    if c == 0:
                                        take_numerator(i, 0)
                                    normalise(i, c, fin_before(i, k) + 1)
                                elif kind == "vt":
                                    scan(i + 1, c)


def feed_forward(nc, x, ot, wt, w_out, b_out, biases, gamma, beta, out):
    n_chunks = x.shape[0]
    D = w_out.shape[1]
    halves = D // P
    n_pairs = w_out.shape[0] // P
    n_blk = gamma.shape[0]
    with ExitStack() as ctx:
        def sb(name, shape, dt=F32):
            return ctx.enter_context(nc.sbuf_tensor(name, shape, dt))

        def sem(name):
            return ctx.enter_context(nc.semaphore(name))

        ident = sb("c_ident", [P, P])
        minus_half = sb("c_minus_half", [P, 4])
        wo = sb("c_wo", [P, n_pairs, D])
        w = sb("c_w", [P, 2 * n_blk, halves, D])
        b_out_row = sb("c_b_out_row", [P, D])
        b1_row = sb("c_b1_row", [P, n_blk, D])
        b2 = sb("c_b2", [P, n_blk, halves])
        ga = sb("c_ga", [P, n_blk, halves])
        be = sb("c_be", [P, n_blk, halves])
        o_in = [sb(f"c_o_in{L}", [P, n_pairs, CH]) for L in range(2)]
        x_in = [sb(f"c_x_in{L}", [P, 4, D]) for L in range(2)]
        xb = [sb(f"c_xb{L}", [P, 4, D]) for L in range(2)]
        x1 = [sb(f"c_x1{L}", [P, 4, D]) for L in range(2)]
        y = [sb(f"c_y{L}", [P, 4, D]) for L in range(2)]
        z = [sb(f"c_z{L}", [P, 4, D]) for L in range(2)]
        ht = [sb(f"c_ht{L}", [P, halves, CH]) for L in range(2)]
        yt = [sb(f"c_yt{L}", [P, halves, CH]) for L in range(2)]
        fin = [sb(f"c_fin{L}", [P, 4, D]) for L in range(2)]
        stats = [sb(f"c_stats{L}", [P, 4, 6]) for L in range(2)]
        mv = [sb(f"c_mv{L}", [P, 4, 2]) for L in range(2)]
        var_eps = [sb(f"c_var{L}", [P, 4]) for L in range(2)]
        rstd = [sb(f"c_rstd{L}", [P, 4]) for L in range(2)]
        ps_y = [ctx.enter_context(nc.psum_tensor(f"c_ps_y{L}", [P, 4, D], F32)) for L in range(2)]
        ps_t = [ctx.enter_context(nc.psum_tensor(f"c_ps_t{L}", [P, halves, CH], F32)) for L in range(2)]

        wait_here = sb("c_wait_here", [P, 1])

        zeroed = sem("c_zeroed")
        ident_ready = sem("c_ident_ready")
        w_loaded = sem("c_w_loaded")
        o_loaded = [sem(f"c_o_loaded{L}") for L in range(2)]
        x_loaded = [sem(f"c_x_loaded{L}") for L in range(2)]
        xb_ready = [sem(f"c_xb_ready{L}") for L in range(2)]
        y_summed = [sem(f"c_y_summed{L}") for L in range(2)]
        y_taken = [sem(f"c_y_taken{L}") for L in range(2)]
        stats_done = [sem(f"c_stats_done{L}") for L in range(2)]
        mv_done = [sem(f"c_mv_done{L}") for L in range(2)]
        var_done = [sem(f"c_var_done{L}") for L in range(2)]
        rstd_done = [sem(f"c_rstd_done{L}") for L in range(2)]
        z_ready = [sem(f"c_z_ready{L}") for L in range(2)]
        z_turned = [sem(f"c_z_turned{L}") for L in range(2)]
        t_taken = [sem(f"c_t_taken{L}") for L in range(2)]
        h_summed = [sem(f"c_h_summed{L}") for L in range(2)]
        h_ready = [sem(f"c_h_ready{L}") for L in range(2)]
        stored = [sem(f"c_stored{L}") for L in range(2)]

        YS = 2 + n_blk
        ZS = 1 + n_blk

        loads = [(wo[:, :, :], w_out.rearrange("(a p) d -> p a d", p=P)),
                 (b_out_row[:, :], b_out.rearrange("(o d) -> o d", o=1).to_broadcast([P, D]))]
        for l in range(2 * n_blk):
            loads.append((w[:, l], wt[l]))
        for k in range(n_blk):
            loads.append((b1_row[:, k, :], biases[2 * k:2 * k + 1, :].to_broadcast([P, D])))
            for s in range(halves):
                half = slice(s * P, (s + 1) * P)
                loads.append((b2[:, k, s:s + 1], biases[2 * k + 1:2 * k + 2, half].rearrange("o p -> p o")))
                loads.append((ga[:, k, s:s + 1], gamma[k:k + 1, half].rearrange("o p -> p o")))
                loads.append((be[:, k, s:s + 1], beta[k:k + 1, half].rearrange("o p -> p o")))

        with nc.Block() as block:
            @block.sync
            def _(sp):
                for dst, src in loads:
                    sp.dma_start(dst, src).then_inc(w_loaded, 16)

                def load(i, L):
                    g = (2 * i + L) % n_chunks
                    sp.dma_start(o_in[L][:, :, :], ot.rearrange("b a c p t -> b c p a t")[g // 4, 3 - g % 4]
                                 ).then_inc(o_loaded[L], 16)
                    sp.dma_start(x_in[L][:, :, :], x[g]).then_inc(x_loaded[L], 16)

                for L in range(2):
                    load(0, L)
                with sp.Fori(0, n_chunks // 2) as i:
                    for L in range(2):
                        sp.wait_ge(xb_ready[L], i + 1)
                        sp.wait_ge(y_summed[L], YS * i + 1)
                        load(i + 1, L)
                    for L in range(2):
                        sp.wait_ge(y_taken[L], YS * i + YS)
                        sp.dma_start(out[2 * i + L], fin[L][:, :, :]).then_inc(stored[L], 16)
                for L in range(2):
                    sp.wait_ge(stored[L], 16 * (n_chunks // 2))
                    sp.wait_ge(o_loaded[L], 16 * (n_chunks // 2 + 1))
                    sp.wait_ge(x_loaded[L], 16 * (n_chunks // 2 + 1))

            @block.gpsimd
            def _(pool):
                nc.gpsimd.memset(ident[:, :], 0.0).then_inc(zeroed, 1)
                nc.gpsimd.memset(minus_half[:, :], -0.5).then_inc(zeroed, 1)
                pool.wait_ge(zeroed, 2)
                nc.gpsimd.affine_select(out=ident[:, :], in_=ident[:, :], compare_op=ALU.not_equal, fill=1.0,
                                        base=0, pattern=[[-1, P]], channel_multiplier=1).then_inc(ident_ready, 1)
                pool.wait_ge(w_loaded, 16 * len(loads))
                with pool.Fori(0, n_chunks // 2) as i:
                    for L in range(2):
                        pool.wait_ge(x_loaded[L], 16 * i + 16)
                        pool.wait_ge(y_taken[L], YS * i)
                        nc.gpsimd.tensor_tensor(xb[L][:, :, :], x_in[L][:, :, :],
                                                b_out_row[:, :].unsqueeze(1).to_broadcast([P, 4, D]),
                                                ALU.add).then_inc(xb_ready[L], 1)
                    for k in range(ZS):
                        for L in range(2):
                            pool.wait_ge(var_done[L], ZS * i + k + 1)
                            nc.gpsimd.tensor_tensor(rstd[L][:, :], var_eps[L][:, :], minus_half[:, :],
                                                    ALU.pow).then_inc(rstd_done[L], 1)

            @block.tensor
            def _(pe):
                pe.wait_ge(ident_ready, 1)
                pe.wait_ge(w_loaded, 16 * len(loads))

                def turn_z(i, k, L):
                    pe.wait_ge(z_ready[L], ZS * i + k + 1)
                    pe.wait_ge(h_ready[L], n_blk * i + max(k - 1, 0))
                    for s in range(halves):
                        for t in range(4):
                            mm = pe.transpose(ps_t[L][:, s, t * P:(t + 1) * P], z[L][:, t, s * P:(s + 1) * P],
                                              ident[:, :])
                    mm.then_inc(z_turned[L], 1)

                with pe.Fori(0, n_chunks // 2) as i:
                    for L in range(2):
                        pe.wait_ge(o_loaded[L], 16 * i + 16)
                        pe.wait_ge(y_taken[L], YS * i)
                        for t in range(4):
                            for a in range(n_pairs):
                                mm = pe.matmul(ps_y[L][:, t, :], o_in[L][:, a, t * P:(t + 1) * P], wo[:, a, :],
                                               start=(a == 0 and t % 2 == 0), stop=(a == n_pairs - 1),
                                               skip_group_check=True)
                        mm.then_inc(y_summed[L], 1)
                    for L in range(2):
                        turn_z(i, 0, L)
                    for k in range(n_blk):
                        for L in range(2):
                            if k == 0:
                                pe.wait_ge(t_taken[L], ZS * i + 1)
                            else:
                                pe.wait_ge(h_ready[L], n_blk * i + k)
                            pe.wait_ge(y_taken[L], YS * i + 1 + k)
                            for t in range(4):
                                for s in range(halves):
                                    mm = pe.matmul(ps_y[L][:, t, :], ht[L][:, s, t * P:(t + 1) * P], w[:, 2 * k, s, :],
                                                   start=(s == 0 and t % 2 == 0), stop=(s == halves - 1),
                                                   skip_group_check=True)
                            mm.then_inc(y_summed[L], 1)
                        for L in range(2):
                            turn_z(i, k + 1, L)
                        for L in range(2):
                            pe.wait_ge(t_taken[L], ZS * i + k + 2)
                            for s in range(halves):
                                for r in range(halves):
                                    mm = pe.matmul(ps_t[L][:, s, :], w[:, 2 * k + 1, r, s * P:(s + 1) * P], yt[L][:, r, :],
                                                   start=(r == 0), stop=(r == halves - 1))
                            mm.then_inc(h_summed[L], 1)
                    for L in range(2):
                        pe.wait_ge(h_ready[L], n_blk * i + n_blk)
                        for t in range(4):
                            for s in range(halves):
                                mm = pe.transpose(ps_y[L][:, t, s * P:(s + 1) * P], ht[L][:, s, t * P:(t + 1) * P],
                                                  ident[:, :])
                        mm.then_inc(y_summed[L], 1)

            @block.scalar
            def _(act):
                act.wait_ge(w_loaded, 16 * len(loads))
                with act.Fori(0, n_chunks // 2) as i:
                    for L in range(2):
                        act.wait_ge(z_turned[L], ZS * i + 1)
                        act.wait_ge(y_summed[L], YS * i)
                        nc.scalar.copy(ht[L][:, :, :], ps_t[L][:, :, :]).then_inc(t_taken[L], 1)
                    for k in range(n_blk):
                        for L in range(2):
                            act.wait_ge(z_turned[L], ZS * i + k + 2)
                            act.wait_ge(h_summed[L], n_blk * i + k)
                            for s in range(halves):
                                a = nc.scalar.activation(yt[L][:, s, :], ps_t[L][:, s, :], ACT.Gelu,
                                                         bias=be[:, k, s:s + 1], scale=ga[:, k, s:s + 1])
                            a.then_inc(t_taken[L], 1)

            @block.vector
            def _(dve):
                e = nc.vector
                dve.wait_ge(w_loaded, 16 * len(loads))

                def normalised(i, k, L, src):
                    n = ZS * i + k
                    dve.wait_ge(y_taken[L], YS * i + k + 1)
                    for t in range(4):
                        e.bn_stats(stats[L][:, t, :], src[:, t, :]).then_inc(stats_done[L], 1)
                    dve.wait_ge(stats_done[L], 4 * n + 4)
                    e.memset(wait_here[:, :], 0.0)
                    for t in range(4):
                        e.bn_aggr(mv[L][:, t, :], stats[L][:, t, :]).then_inc(mv_done[L], 1)
                    dve.wait_ge(mv_done[L], 4 * n + 4)
                    e.tensor_scalar(var_eps[L][:, :], mv[L][:, :, 1], LN_EPS, None, ALU.add).then_inc(var_done[L], 1)

                def scaled(i, k, L, src):
                    n = ZS * i + k
                    dve.wait_ge(rstd_done[L], n + 1)
                    dve.wait_ge(z_turned[L], n)
                    for t in range(4):
                        a = e.tensor_scalar(z[L][:, t, :], src[:, t, :], mv[L][:, t, 0:1], rstd[L][:, t:t + 1],
                                            ALU.subtract, ALU.mult)
                    a.then_inc(z_ready[L], 1)

                with dve.Fori(0, n_chunks // 2) as i:
                    for L in range(2):
                        dve.wait_ge(y_summed[L], YS * i + 1)
                        dve.wait_ge(xb_ready[L], i + 1)
                        e.tensor_tensor(x1[L][:, :, :], ps_y[L][:, :, :], xb[L][:, :, :], ALU.add).then_inc(y_taken[L], 1)
                        normalised(i, 0, L, x1[L])
                    for L in range(2):
                        scaled(i, 0, L, x1[L])
                    for k in range(n_blk):
                        for L in range(2):
                            dve.wait_ge(y_summed[L], YS * i + 2 + k)
                            e.tensor_tensor(y[L][:, :, :], ps_y[L][:, :, :],
                                            b1_row[:, k, :].unsqueeze(1).to_broadcast([P, 4, D]),
                                            ALU.add).then_inc(y_taken[L], 1)
                            normalised(i, k + 1, L, y[L])
                        for L in range(2):
                            scaled(i, k + 1, L, y[L])
                        for L in range(2):
                            dve.wait_ge(h_summed[L], n_blk * i + k + 1)
                            for s in range(halves):
                                a = e.scalar_tensor_tensor(ht[L][:, s, :], ps_t[L][:, s, :], b2[:, k, s:s + 1],
                                                           ht[L][:, s, :], ALU.add, ALU.add)
                            a.then_inc(h_ready[L], 1)
                    for L in range(2):
                        dve.wait_ge(y_summed[L], YS * i + YS)
                        dve.wait_ge(stored[L], 16 * i)
                        e.tensor_tensor(fin[L][:, :, :], ps_y[L][:, :, :], x1[L][:, :, :], ALU.add
                                        ).then_inc(y_taken[L], 1)


def program(nc, residual, w_key, w_query, w_values, w_output, b_key, b_query, b_values, b_output,
            qweights, scales, biases, lora_a, lora_b, ln_gamma, ln_beta, out):
    B, S, D = residual.shape
    n_heads, _, H = w_key.shape
    n_chunks = B * S // CH
    halves = D // P
    n_pairs = n_heads // 2
    xnt = nc.dram_tensor("xn_turned", [n_chunks, P, halves, CH], F32).ap()
    wt = nc.dram_tensor("weights_turned", [qweights.shape[0], P, halves, D], F32).ap()
    ot = nc.dram_tensor("heads_turned", [B, n_pairs, 4, P, CH], F32).ap()
    x = residual.rearrange("b (c t p) d -> (b c) p t d", c=S // CH, p=P)
    y = out.rearrange("b (c t p) d -> (b c) p t d", c=S // CH, p=P)
    layernorm_and_weights(nc, x, qweights, scales, lora_a, lora_b, xnt, wt)
    attention(nc, xnt, [w_query, w_key, w_values], [b_query, b_key, b_values], ot)
    feed_forward(nc, x, ot, wt, w_output.rearrange("n h e -> (n h) e"), b_output, biases, ln_gamma, ln_beta, y)


_INS = ["L0_attn_residual", "L0_attn_W_key", "L0_attn_W_query", "L0_attn_W_values", "L0_attn_W_output",
        "L0_attn_Bias_key", "L0_attn_Bias_query", "L0_attn_Bias_values", "L0_attn_Bias_output",
        "L0_ffn_qweights", "L0_ffn_scales", "L0_ffn_biases", "L0_ffn_lora_a", "L0_ffn_lora_b",
        "L0_ffn_ln_gamma", "L0_ffn_ln_beta"]


def kernel(**inputs):
    import concourse.bacc as bacc
    from concourse.bass_utils import run_bass_kernel_spmd as run

    nc = bacc.Bacc("TRN2", target_bir_lowering=False, num_devices=1)
    arrays, args = {}, []
    for name in _INS:
        a = np.ascontiguousarray(inputs[name])
        arrays[f"in_{name}"] = a
        args.append(nc.dram_tensor(f"in_{name}", a.shape, mybir.dt.from_np(a.dtype), kind="ExternalInput").ap())
    shape = arrays["in_L0_attn_residual"].shape
    args.append(nc.dram_tensor("out_0", shape, F32, kind="ExternalOutput").ap())
    program(nc, *args)
    r = run(nc, [arrays], core_ids=[0])
    return r.results[0]["out_0"]
```

```python
from contextlib import ExitStack

import numpy as np

import concourse.bass as bass
from concourse import mybir

F32 = mybir.dt.float32
F32R = mybir.dt.float32r
BF16 = mybir.dt.bfloat16
I32 = mybir.dt.int32
ALU = mybir.AluOpType
ACT = mybir.ActivationFunctionType
AX = mybir.AxisListType

P = 128
CH = 512
SCORE_SCALE = 0.125
MASKED_RAW = 8e-10
MASKED = 1e-10
NEVER = -1e30
LN_EPS = 1e-5


START = 1


def start_counts(nc, sems):
    with nc.Block() as block:
        @block.sync
        def _(sp):
            for s in sems:
                sp.sem_inc(s, START)


def layernorm_and_weights(nc, x, qweights, scales, lora_a, lora_b, xnt, wt):
    n_layers, _, D = qweights.shape
    R = lora_a.shape[1]
    n_chunks = x.shape[0]
    halves = D // P
    groups = D // 16
    with ExitStack() as ctx:
        def sb(name, shape, dt=F32):
            return ctx.enter_context(nc.sbuf_tensor(name, shape, dt))

        sems = []

        def sem(name):
            sems.append(ctx.enter_context(nc.semaphore(name)))
            return sems[-1]

        ident = sb("a_ident", [P, P])
        minus_half = sb("a_minus_half", [P, 4])
        q_in = sb("a_q_in", [P, n_layers, halves, D], I32)
        sc_in = sb("a_sc_in", [P, n_layers, halves, groups])
        la_in = sb("a_la_in", [R, n_layers, D])
        lb_in = sb("a_lb_in", [P, n_layers, halves, R])
        w_unit = sb("a_w_unit", [P, n_layers, halves, D])
        w_deq = sb("a_w_deq", [P, n_layers, halves, D])
        lbt = sb("a_lbt", [R, 2, D])
        w_t = sb("a_w_t", [P, n_layers, halves * D])
        x_in = sb("a_x_in", [P, 2, 4, D])
        stats = sb("a_stats", [P, 2, 4, 6])
        mv = sb("a_mv", [P, 2, 4, 2])
        wait_here = sb("a_wait_here", [P, 1])
        var_eps = sb("a_var_eps", [P, 2, 4])
        rstd = sb("a_rstd", [P, 2, 4])
        xn = sb("a_xn", [P, 2, 4, D])
        xt = sb("a_xt", [P, 2, halves, CH])
        ps_w = ctx.enter_context(nc.psum_tensor("a_ps_w", [P, 2, halves * D], F32))
        ps_b = ctx.enter_context(nc.psum_tensor("a_ps_b", [P, CH], F32))
        ps_x = ctx.enter_context(nc.psum_tensor("a_ps_x", [P, 2, halves, CH], F32))

        ident_zero = sem("a_ident_zero")
        ident_ready = sem("a_ident_ready")
        w_loaded = sem("a_w_loaded")
        w_units = sem("a_w_units")
        w_dequant = sem("a_w_dequant")
        lb_turned = sem("a_lb_turned")
        lbt_ready = sem("a_lbt_ready")
        w_summed = sem("a_w_summed")
        wt_ready = sem("a_wt_ready")
        wt_stored = sem("a_wt_stored")
        x_loaded = [sem(f"a_x_loaded{b}") for b in range(2)]
        stats_done = sem("a_stats_done")
        mv_done = sem("a_mv_done")
        var_done = sem("a_var_done")
        rstd_done = sem("a_rstd_done")
        xn_done = sem("a_xn_done")
        x_turned = sem("a_x_turned")
        xt_ready = sem("a_xt_ready")
        xt_stored = [sem(f"a_xt_stored{b}") for b in range(2)]

        start_counts(nc, sems)
        with nc.Block() as block:
            @block.sync
            def _(sp):
                for b in range(2):
                    sp.dma_start(x_in[:, b], x[b]).then_inc(x_loaded[b], 16)
                for l in range(n_layers):
                    sp.dma_start(q_in[:, l], qweights[l].rearrange("(h p) d -> p h d", p=P)).then_inc(w_loaded, 16)
                    sp.dma_start(sc_in[:, l], scales[l].rearrange("(h p) g -> p h g", p=P)).then_inc(w_loaded, 16)
                    sp.dma_start(la_in[:, l], lora_a[l]).then_inc(w_loaded, 16)
                    sp.dma_start(lb_in[:, l], lora_b[l].rearrange("(h p) r -> p h r", p=P)).then_inc(w_loaded, 16)
                for l in range(n_layers):
                    sp.wait_ge(wt_ready, START + l + 1)
                    sp.dma_start(wt[l], w_t[:, l].rearrange("p (h d) -> p h d", h=halves)).then_inc(wt_stored, 16)
                with sp.Fori(0, n_chunks // 2) as i:
                    for b in range(2):
                        sp.wait_ge(xt_ready, START + 2 * i + b + 1)
                        sp.dma_start(xnt[2 * i + b], xt[:, b]).then_inc(xt_stored[b], 16)
                        sp.dma_start(x_in[:, b], x[(2 * i + b + 2) % n_chunks]).then_inc(x_loaded[b], 16)
                sp.wait_ge(wt_stored, START + 16 * n_layers)
                for b in range(2):
                    sp.wait_ge(xt_stored[b], START + 16 * (n_chunks // 2))
                    sp.wait_ge(x_loaded[b], START + 16 * (n_chunks // 2 + 1))

            @block.gpsimd
            def _(pool):
                nc.gpsimd.memset(ident[:, :], 0.0).then_inc(ident_zero, 1)
                nc.gpsimd.memset(minus_half[:, :], -0.5).then_inc(ident_zero, 1)
                pool.wait_ge(ident_zero, START + 2)
                nc.gpsimd.affine_select(out=ident[:, :], in_=ident[:, :], compare_op=ALU.not_equal, fill=1.0,
                                        base=0, pattern=[[-1, P]], channel_multiplier=1).then_inc(ident_ready, 1)
                with pool.Fori(0, n_chunks // 2) as i:
                    for b in range(2):
                        pool.wait_ge(var_done, START + 2 * i + b + 1)
                        nc.gpsimd.tensor_tensor(rstd[:, b], var_eps[:, b], minus_half[:, :],
                                                ALU.pow).then_inc(rstd_done, 1)

            @block.vector
            def _(dve):
                dve.wait_ge(w_loaded, START + 64 * n_layers)
                nc.vector.tensor_scalar(w_unit[:, :, :, :], q_in[:, :, :, :], 1.0 / 7.5, -1.0,
                                        ALU.mult, ALU.add).then_inc(w_units, 1)
                dve.wait_ge(w_units, START + 1)
                nc.vector.tensor_tensor(
                    w_deq[:, :, :, :].rearrange("p l h (g e) -> p (l h g) e", e=16),
                    w_unit[:, :, :, :].rearrange("p l h (g e) -> p (l h g) e", e=16),
                    sc_in[:, :, :, :].rearrange("p l h g -> p (l h g)").unsqueeze(2).to_broadcast(
                        [P, n_layers * halves * groups, 16]), ALU.mult).then_inc(w_dequant, 1)
                with dve.Fori(0, n_chunks // 2) as i:
                    for b in range(2):
                        dve.wait_ge(x_loaded[b], START + 16 * i + 16)
                        for t in range(4):
                            nc.vector.bn_stats(stats[:, b, t, :], x_in[:, b, t, :]).then_inc(stats_done, 1)
                        dve.wait_ge(stats_done, START + 8 * i + 4 * b + 4)
                        nc.vector.memset(wait_here[:, :], 0.0)
                        for t in range(4):
                            nc.vector.bn_aggr(mv[:, b, t, :], stats[:, b, t, :]).then_inc(mv_done, 1)
                        dve.wait_ge(mv_done, START + 8 * i + 4 * b + 4)
                        nc.vector.tensor_scalar(var_eps[:, b], mv[:, b, :, 1], LN_EPS, None,
                                                ALU.add).then_inc(var_done, 1)
                        dve.wait_ge(rstd_done, START + 2 * i + b + 1)
                        dve.wait_ge(x_turned, START + 2 * i)
                        for t in range(4):
                            last = nc.vector.tensor_scalar(xn[:, b, t, :], x_in[:, b, t, :], mv[:, b, t, 0:1],
                                                           rstd[:, b, t:t + 1], ALU.subtract, ALU.mult)
                        last.then_inc(xn_done, 1)

            @block.tensor
            def _(pe):
                pe.wait_ge(ident_ready, START + 1)
                def turn_lora_b(l):
                    if l >= 1:
                        pe.wait_ge(lbt_ready, START + l)
                    for h in range(halves):
                        mm = pe.matmul(ps_b[0:R, h * P:(h + 1) * P], lb_in[:, l, h, :], ident[:, :],
                                       start=(h == 0), stop=True, skip_group_check=True)
                    mm.then_inc(lb_turned, 1)

                pe.wait_ge(w_loaded, START + 64 * n_layers)
                turn_lora_b(0)
                pe.wait_ge(w_dequant, START + 1)
                for l in range(n_layers):
                    if l >= 2:
                        pe.wait_ge(wt_ready, START + l - 1)
                    for s in range(halves):
                        for h in range(halves):
                            at = s * D + h * P
                            pe.matmul(ps_w[:, l % 2, at:at + P], w_deq[:, l, h, s * P:(s + 1) * P], ident[:, :],
                                      start=(s == 0 and h == 0), stop=False, skip_group_check=True)
                    if l + 1 < n_layers:
                        turn_lora_b(l + 1)
                    pe.wait_ge(lbt_ready, START + l + 1)
                    for s in range(halves):
                        mm = pe.matmul(ps_w[:, l % 2, s * D:(s + 1) * D], la_in[:, l, s * P:(s + 1) * P],
                                       lbt[:, l % 2], start=False, stop=True, skip_group_check=True)
                    mm.then_inc(w_summed, 1)
                with pe.Fori(0, n_chunks // 2) as i:
                    for b in range(2):
                        pe.wait_ge(xn_done, START + 2 * i + b + 1)
                        pe.wait_ge(xt_ready, START + 2 * i)
                        for s in range(halves):
                            for t in range(4):
                                mm = pe.transpose(ps_x[:, b, s, t * P:(t + 1) * P],
                                                  xn[:, b, t, s * P:(s + 1) * P], ident[:, :])
                        mm.then_inc(x_turned, 1)

            @block.scalar
            def _(act):
                def take_lora_b(l):
                    act.wait_ge(lb_turned, START + l + 1)
                    if l >= 2:
                        act.wait_ge(w_summed, START + l - 1)
                    nc.scalar.copy(lbt[:, l % 2], ps_b[0:R, 0:D]).then_inc(lbt_ready, 1)

                take_lora_b(0)
                for l in range(n_layers):
                    if l + 1 < n_layers:
                        take_lora_b(l + 1)
                    act.wait_ge(w_summed, START + l + 1)
                    nc.scalar.copy(w_t[:, l], ps_w[:, l % 2]).then_inc(wt_ready, 1)
                with act.Fori(0, n_chunks // 2) as i:
                    for b in range(2):
                        act.wait_ge(x_turned, START + 2 * i + b + 1)
                        act.wait_ge(xt_stored[b], START + 16 * i)
                        nc.scalar.copy(xt[:, b], ps_x[:, b]).then_inc(xt_ready, 1)


def tiles_of(group):
    order = [1, 2, 3, 0] if group == 3 else list(range(group + 1))
    out = []
    for chunk in order:
        for half in range(2):
            tile, at = [], 0
            for r in (2 * half, 2 * half + 1):
                q0 = 128 * r if chunk == group else 0
                w = CH - q0
                if at and at + w > CH:
                    at = CH
                tile.append((4 * chunk + r, q0, w, at))
                at += w
            out.append(tile)
    return out


GROUPS = [3, 2, 1, 0]
TILES = [(g, tile) for g in GROUPS for tile in tiles_of(g)]
NT = len(TILES)
FIRST_TILE = {g: min(t for t in range(NT) if TILES[t][0] == g) for g in GROUPS}
LAST_TILE = {g: max(t for t in range(NT) if TILES[t][0] == g) for g in GROUPS}
GAP = 2
SLOTS = 6 * NT
NP_SLOTS = 3


def pool_ops_before(t):
    n = 0
    for k in range(min(t, LAST_TILE[1] + 1)):
        n += 2 if k == FIRST_TILE[TILES[k][0]] else 4
    return n


POOL_OPS = pool_ops_before(NT)


def slot_user_before(t):
    if t >= NP_SLOTS:
        return 0, t - NP_SLOTS
    return 1, max(k for k in range(NT) if k % NP_SLOTS == t % NP_SLOTS)


MAX_UNITS = [(h, qb, u, min(CH, 128 * (qb + 1) - CH * u))
             for c in GROUPS for qb in range(4 * c + 3, 4 * c - 1, -1) for u in range(c + 1) for h in range(2)]
NMAX = len(MAX_UNITS)
NPROJ = 12
PROJ_SLOT = [3 * u for u in range(NPROJ)]
MAX_SLOT = 35
LAST_MAX = {c: max(v for v in range(NMAX) if MAX_UNITS[v][1] // 4 == c) for c in GROUPS}

FIN = [("vt", 0, 3), ("bc", 3, 30), ("vt", 3, 50), ("den", 3, 60), ("bc", 2, 68), ("mt", 3, 72), ("vt", 2, 86),
       ("mt", 2, 96), ("den", 2, 98), ("bc", 1, 101), ("den", 1, 110), ("vt", 1, 112), ("mt", 1, 114),
       ("bc", 0, 118), ("mt", 0, 119), ("den", 0, SLOTS)]
NFIN = len(FIN)


def values_pair(i, kind, c):
    return i if (kind, c) == ("vt", 0) else i + 1


FIN_FIRST = [("mt", 3), ("mt", 2), ("mt", 1), ("mt", 0), ("vt", 3), ("vt", 2), ("vt", 1)]
NFIRST = len(FIN_FIRST)


def attention(nc, xnt, w_qkv, b_qkv, ot):
    n_chunks, _, halves, _ = xnt.shape
    n_b = n_chunks // 4
    n_pairs = w_qkv[0].shape[0] // 2
    N = n_b * n_pairs
    S = 4 * CH
    with ExitStack() as ctx:
        def sb(name, shape, dt=F32):
            return ctx.enter_context(nc.sbuf_tensor(name, shape, dt))

        sems = []

        def sem(name):
            sems.append(ctx.enter_context(nc.semaphore(name)))
            return sems[-1]

        ident = sb("ident", [P, P])
        ident_bf = sb("ident_bf", [P, P], BF16)
        never_above = sb("never_above", [P, P], BF16)
        mask_q = sb("mask_q", [P, CH])
        ones64 = sb("ones64", [P, 64])
        ones_row = sb("ones_row", [P, CH], BF16)
        select = sb("select", [P, 2, P], F32R)
        keys_after = sb("keys_after", [P, CH])
        masked_bias = sb("masked_bias", [P, 1])

        w_in = sb("w_in", [P, halves, 3, P])
        bias = sb("bias", [P, 3])
        xs = sb("xs", [P, 2, halves, CH])
        hi = [sb(f"hi_{m}", [P, S], F32R) for m in "qk"]
        lo = [sb(f"lo_{m}", [P, S], F32R) for m in "qk"]
        vt = sb("vt", [P, S])
        q_pad = [sb(f"q_pad{h}", [P, S], BF16) for h in range(2)]
        k_bf = sb("k_bf", [P, S], BF16)
        partial = sb("partial", [P, 2, 16, 5])
        neg_max = sb("neg_max", [P, 4, 8])
        m_row = sb("m_row", [8, 4, P], F32R)
        junk = sb("junk", [P, 2, CH], BF16)
        wait_here = sb("wait_here", [P, 4])

        qq = [sb(f"qq{h}", [P, S], F32R) for h in range(2)]
        qm = [sb(f"qm{h}", [P, S], F32R) for h in range(2)]
        kk = [sb(f"kk{h}", [P, S], F32R) for h in range(2)]
        kl = [sb(f"kl{h}", [P, S], F32R) for h in range(2)]
        v = sb("v", [P, 16, P])
        v_sum = sb("v_sum", [P, S])
        v_tail = sb("v_tail", [P, 5])
        probs = [sb(f"probs{h}", [P, NP_SLOTS, 2 * CH]) for h in range(2)]
        acc = [sb(f"acc{h}", [P, 2, CH]) for h in range(2)]
        e0 = sb("e0", [P, CH])
        masked_num = sb("masked_num", [P, CH])
        masked_den = sb("masked_den", [P, CH])
        num = sb("num", [P, CH])
        den = sb("den", [P, CH])
        o_out = sb("o_out", [P, 2, CH])

        ps_s = ctx.enter_context(nc.psum_tensor("ps_s", [P, 2, 2 * CH], F32))
        ps_bg = ctx.enter_context(nc.psum_tensor("ps_bg", [P, 2, CH], F32))
        ps_o = ctx.enter_context(nc.psum_tensor("ps_o", [P, CH], F32))
        ps_fin = ctx.enter_context(nc.psum_tensor("ps_fin", [P, CH], F32))

        zeroed = sem("zeroed")
        shaped = sem("shaped")
        set_up = sem("set_up")
        consts = sem("consts")
        counted = sem("counted")
        w_loaded = sem("w_loaded")
        xs_loaded = [sem(f"xs_loaded{b}") for b in range(2)]
        proj_done = sem("proj_done")
        hi_ready = sem("hi_ready")
        proj_read = sem("proj_read")
        bf_ready = sem("bf_ready")
        max_scores = sem("max_scores")
        max_read = sem("max_read")
        max_ready = sem("max_ready")
        stack_in = [sem(f"stack_in{c}") for c in range(4)]
        row_in = [sem(f"row_in{c}") for c in range(4)]
        fin_written = sem("fin_written")
        fin_read = sem("fin_read")
        s_ready = sem("s_ready")
        p_ready = sem("p_ready")
        pv_done = sem("pv_done")
        added = sem("added")
        sums_ready = sem("sums_ready")
        tail_ready = sem("tail_ready")
        e0_ready = sem("e0_ready")
        step = sem("step")
        num_ready = sem("num_ready")
        o_ready = sem("o_ready")
        o_stored = [sem(f"o_stored{b}") for b in range(2)]

        def cols(c):
            return slice(CH * c, CH * (c + 1))

        def fin_before(i, k):
            return NFIN * i + NFIRST + k

        def fin_index(kind, c):
            return [e[:2] for e in FIN].index((kind, c))

        start_counts(nc, sems)
        with nc.Block() as block:
            @block.sync
            def _(sp):
                def load_weights(j):
                    sp.wait_ge(proj_read, START + NPROJ * j)
                    pair = j % n_pairs
                    for m in range(3):
                        for s in range(halves):
                            sp.dma_start(w_in[:, s, m, :].rearrange("p (n h) -> p n h", n=2),
                                         w_qkv[m].rearrange("(a n) (s p) h -> a s p n h", n=2, p=P)[pair, s]
                                         ).then_inc(w_loaded, 16)
                        sp.dma_start(bias[:, m:m + 1],
                                     b_qkv[m].rearrange("(a n) (h o) -> a (n h) o", n=2, o=1)[pair]
                                     ).then_inc(w_loaded, 16)

                def load_x(j, c):
                    sp.wait_ge(proj_done, START + NPROJ * j + (3 * (c - 1) if c >= 2 else 0))
                    sp.dma_start(xs[:, c % 2], xnt[4 * ((j // n_pairs) % n_b) + c]).then_inc(xs_loaded[c % 2], 16)

                def install(j, c):
                    sp.wait_ge(proj_read, START + NPROJ * (j + 1))
                    for h in range(2):
                        own = slice(64 * h, 64 * h + 64)
                        for dst, rows, src in ((qq[h], slice(0, 64), hi[0]), (qq[h], slice(64, 128), lo[0]),
                                               (qm[h], slice(0, 64), hi[0]), (kk[h], slice(0, 64), hi[1]),
                                               (kk[h], slice(64, 128), hi[1]), (kl[h], slice(0, 64), lo[1])):
                            sp.dma_start(dst[rows, cols(c)].bitcast(F32), src[own, cols(c)].bitcast(F32)
                                         ).then_inc(stack_in[c], 16)

                def install_max(c, written):
                    sp.wait_ge(fin_read, START + written)
                    for h in range(2):
                        for r in range(4):
                            at = CH * c + P * r
                            sp.dma_start(qm[h][64:65, at:at + P].bitcast(F32),
                                         m_row[4 * h + r:4 * h + r + 1, c, :].bitcast(F32)).then_inc(row_in[c], 16)

                load_weights(0)
                for c in range(4):
                    load_x(0, c)
                sp.wait_ge(consts, START + 1)
                for c in GROUPS:
                    install(0, c)
                load_weights(1)
                for c in range(2):
                    load_x(1, c)
                for k, (kind, c) in enumerate(FIN_FIRST):
                    if kind == "mt":
                        install_max(c, k + 1)
                with sp.Fori(0, N) as i:
                    for c in (2, 3):
                        load_x(i + 1, c)
                    load_weights(i + 2)
                    for c in (0, 1):
                        load_x(i + 2, c)
                    for c in GROUPS:
                        sp.wait_ge(pv_done, START + NT * i + LAST_TILE[c] + 1)
                        install(i + 1, c)
                        install_max(c, fin_before(i, fin_index("mt", c)) + 1)
                        sp.wait_ge(o_ready, START + 4 * i + (3 - c) + 1)
                        sp.dma_start(ot[i // n_pairs, i % n_pairs, 3 - c], o_out[:, c % 2]).then_inc(o_stored[c % 2], 16)
                for b in range(2):
                    sp.wait_ge(o_stored[b], START + 16 * 2 * N)
                    sp.wait_ge(xs_loaded[b], START + 16 * (2 * N + 3))
                for c in range(4):
                    sp.wait_ge(stack_in[c], START + 192 * (N + 1))
                    sp.wait_ge(row_in[c], START + 128 * (N + 1))
                sp.wait_ge(w_loaded, START + 144 * (N + 2))

            @block.gpsimd
            def _(pool):
                g = nc.gpsimd
                for tile in (ident, ident_bf, never_above, mask_q):
                    g.memset(tile[:, :], 0.0).then_inc(zeroed, 1)
                pool.wait_ge(zeroed, START + 4)
                for tile in (ident, ident_bf):
                    g.affine_select(out=tile[:, :], in_=tile[:, :], compare_op=ALU.not_equal, fill=1.0,
                                    base=0, pattern=[[-1, P]], channel_multiplier=1).then_inc(shaped, 1)
                g.affine_select(out=never_above[:, :], in_=never_above[:, :], compare_op=ALU.is_ge, fill=NEVER,
                                base=0, pattern=[[1, P]], channel_multiplier=-1).then_inc(shaped, 1)
                tri = mask_q[:, CH - P:CH]
                g.affine_select(out=tri, in_=tri, compare_op=ALU.is_ge, fill=NEVER,
                                base=0, pattern=[[-1, P]], channel_multiplier=1).then_inc(shaped, 1)
                pool.wait_ge(counted, START + 1)
                for h in range(2):
                    col = partial[:, h, 15, 4:5]
                    g.affine_select(out=col, in_=col, compare_op=ALU.not_equal, fill=NEVER,
                                    base=-(P - 1), pattern=[[0, 1]], channel_multiplier=1).then_inc(shaped, 1)
                with pool.Fori(0, N) as i:
                    n = 0
                    for t in range(LAST_TILE[1] + 1):
                        group, tile = TILES[t]
                        pool.wait_ge(p_ready, START + 2 * NT * i + 2 * t + 2)
                        if t == FIRST_TILE[group]:
                            if group == 1:
                                pool.wait_ge(fin_written, START + fin_before(i, fin_index("den", 3)) + 1)
                            else:
                                pool.wait_ge(fin_written, START + fin_before(i, 0))
                            for h in range(2):
                                pr = probs[h][:, t % NP_SLOTS]
                                g.tensor_tensor(acc[h][:, group % 2, :], pr[:, 0:CH], pr[:, CH:2 * CH], ALU.add).then_inc(added, 1)
                            n += 2
                            continue
                        for kb, q0, w, at in tile:
                            for h in range(2):
                                pool.wait_ge(added, START + POOL_OPS * i + n - 1)
                                g.tensor_tensor(acc[h][:, group % 2, q0:q0 + w], acc[h][:, group % 2, q0:q0 + w],
                                                probs[h][:, t % NP_SLOTS, at:at + w], ALU.add).then_inc(added, 1)
                                n += 1

            @block.tensor
            def _(pe):
                def project(j, u):
                    c, m = divmod(u, 3)
                    if u == 0:
                        pe.wait_ge(w_loaded, START + 144 * (j + 1))
                        pe.wait_ge(max_read, START + NMAX * j)
                    if m == 0:
                        pe.wait_ge(xs_loaded[c % 2], START + 16 * (2 * j + c // 2 + 1))
                    if u >= 2:
                        pe.wait_ge(proj_read, START + NPROJ * j + u - 1)
                    for s in range(halves):
                        mm = pe.matmul(ps_bg[:, u % 2, :], w_in[:, s, m, :], xs[:, c % 2, s, :],
                                       start=(s == 0), stop=(s == halves - 1))
                    mm.then_inc(proj_done, 1)

                def max_unit(j, n):
                    h, qb, u, w = MAX_UNITS[n]
                    if n == 0:
                        pe.wait_ge(bf_ready, START + 4 * (j + 1))
                    if n < 2:
                        pe.wait_ge(proj_read, START + NPROJ * (j + 1))
                    else:
                        pe.wait_ge(max_read, START + NMAX * j + n - 1)
                    pe.matmul(ps_bg[:, n % 2, 0:w], q_pad[h][:, qb * P:(qb + 1) * P], k_bf[:, CH * u:CH * u + w],
                              start=True, stop=True).then_inc(max_scores, 1)

                def turn_max(j, c, before):
                    pe.wait_ge(max_ready, START + 4 * j + (3 - c) + 1)
                    pe.wait_ge(fin_read, START + before)
                    pe.matmul(ps_fin[0:8, 0:P], neg_max[:, c, :], ident[:, :],
                              start=True, stop=True).then_inc(fin_written, 1)

                def turn_values(c, before):
                    pe.wait_ge(fin_read, START + before)
                    for r in range(4):
                        mm = pe.transpose(ps_fin[:, r * P:(r + 1) * P], vt[:, CH * c + r * P:CH * c + (r + 1) * P],
                                          ident[:, :])
                    mm.then_inc(fin_written, 1)

                def spread_max(group, before):
                    pe.wait_ge(fin_read, START + before)
                    for h in range(2):
                        mm = pe.matmul(ps_fin[:, :], select[:, h, :], qm[h][:, cols(group)],
                                       start=(h == 0), stop=(h == 1))
                    mm.then_inc(fin_written, 1)

                def denominators(i, group, before):
                    pe.wait_ge(fin_read, START + before)
                    if group:
                        pe.wait_ge(added, START + POOL_OPS * i + pool_ops_before(LAST_TILE[group] + 1))
                        for h in range(2):
                            mm = pe.matmul(ps_fin[64 * h:64 * h + 64, :], ones64[:, :], acc[h][:, group % 2, :],
                                           start=True, stop=True, skip_group_check=True)
                    else:
                        for t in range(FIRST_TILE[0], NT):
                            for kb, q0, w, at in TILES[t][1]:
                                for h in range(2):
                                    mm = pe.matmul(ps_fin[64 * h:64 * h + 64, q0:q0 + w], ones64[:, :],
                                                   probs[h][:, t % NP_SLOTS, at:at + w],
                                                   start=(kb == 0), stop=(kb == 3), skip_group_check=True)
                    mm.then_inc(fin_written, 1)

                def scores_wait(i, t, h):
                    group, tile = TILES[t]
                    if h == 0 and t == FIRST_TILE[group]:
                        pe.wait_ge(row_in[group], START + 128 * (i + 1))
                    if h == 0 and t == 0:
                        for c in (3, 2, 1):
                            pe.wait_ge(stack_in[c], START + 192 * (i + 1))
                    if h == 0 and t == LAST_TILE[3] - 1:
                        pe.wait_ge(stack_in[0], START + 192 * (i + 1))

                def scores(t, h, n):
                    group, tile = TILES[t]
                    kb, q0, w, at = tile[n]
                    q = slice(CH * group + q0, CH * (group + 1))
                    diagonal = kb // 4 == group
                    out = ps_s[:, h, at:at + w]
                    pe.matmul(out, kk[h][:, kb * P:(kb + 1) * P], qq[h][:, q], start=True, stop=False,
                              skip_group_check=True)
                    mm = pe.matmul(out, kl[h][:, kb * P:(kb + 1) * P], qm[h][:, q], start=False,
                                   stop=not diagonal, skip_group_check=True)
                    if diagonal:
                        mm = pe.matmul(ps_s[:, h, at:at + P], ident_bf[:, :], never_above[:, :], start=False,
                                       stop=True, skip_group_check=True)
                    if n == 1:
                        mm.then_inc(s_ready, 1)

                def weighted(i, t, n):
                    group, tile = TILES[t]
                    kb, q0, w, at = tile[n]
                    if n == 0:
                        pe.wait_ge(p_ready, START + 2 * NT * i + 2 * t + 2)
                        if t == FIRST_TILE[group]:
                            pe.wait_ge(num_ready, START + 4 * i + (3 - group))
                    first = t == FIRST_TILE[group] and n == 0
                    last = t == LAST_TILE[group] and n == 1
                    for h in range(2):
                        mm = pe.matmul(ps_o[64 * h:64 * h + 64, q0:q0 + w], v[:, kb, 64 * h:64 * h + 64],
                                       probs[h][:, t % NP_SLOTS, at:at + w], start=first, stop=last,
                                       skip_group_check=True)
                    if n == 1:
                        mm.then_inc(pv_done, 1)

                def between(i, n):
                    for u in range(NPROJ):
                        if PROJ_SLOT[u] == n:
                            project(i + 1, u)
                    if MAX_SLOT <= n < MAX_SLOT + NMAX:
                        max_unit(i + 1, n - MAX_SLOT)
                    for k, (kind, c, at) in enumerate(FIN):
                        if at != n:
                            continue
                        before = fin_before(i, k)
                        if kind == "bc":
                            spread_max(c, before)
                        elif kind == "vt":
                            turn_values(c, before)
                        elif kind == "den":
                            denominators(i, c, before)
                        else:
                            turn_max(i + 1, c, before)

                for u in range(NPROJ):
                    project(0, u)
                pe.wait_ge(consts, START + 1)
                for n in range(NMAX):
                    max_unit(0, n)
                for k, (kind, c) in enumerate(FIN_FIRST):
                    if kind == "mt":
                        turn_max(0, c, k)
                    else:
                        turn_values(c, k)
                for h in range(2):
                    scores_wait(0, 0, h)
                    for n in range(2):
                        scores(0, h, n)
                with pe.Fori(0, N) as i:
                    for t in range(NT):
                        ni, nt = (i, t + 1) if t < NT - 1 else (i + 1, 0)
                        for h in range(2):
                            scores_wait(ni, nt, h)
                            pe.wait_ge(p_ready, START + 2 * NT * i + 2 * t + h + 1)
                            for n in range(2):
                                scores(nt, h, n)
                                between(i, 6 * t + 2 * h + n)
                        for n in range(2):
                            weighted(i, t, n)
                            between(i, 6 * t + 4 + n)
                    between(i, SLOTS)

            @block.scalar
            def _(act):
                def high(j, u):
                    c, m = divmod(u, 3)
                    if m == 2:
                        return
                    act.wait_ge(proj_done, START + NPROJ * j + u + 1)
                    act.wait_ge(stack_in[c], START + 192 * j)
                    nc.scalar.activation(hi[m][:, cols(c)], ps_bg[:, u % 2, :], ACT.Identity,
                                         bias=bias[:, m:m + 1]).then_inc(hi_ready, 1)

                def evacuate(j, kind, c, written):
                    act.wait_ge(fin_written, START + written)
                    if kind == "vt":
                        nc.scalar.copy(v[:, 4 * c:4 * c + 4, :].rearrange("p b h -> p (b h)"), ps_fin[:, :]
                                       ).then_inc(fin_read, 1)
                    elif kind == "mt":
                        act.wait_ge(row_in[c], START + 128 * j)
                        nc.scalar.copy(m_row[:, c, :], ps_fin[0:8, 0:P]).then_inc(fin_read, 1)

                def masked_weight(i, group, written):
                    act.wait_ge(fin_written, START + written)
                    act.wait_ge(step, START + 3 * (4 * i + 3 - group))
                    nc.scalar.activation(e0[:, :], ps_fin[:, :], ACT.Exp, bias=masked_bias[:, 0:1],
                                         scale=SCORE_SCALE).then_inc(fin_read, 1)

                act.wait_ge(w_loaded, START + 144)
                for u in range(NPROJ):
                    high(0, u)
                act.wait_ge(consts, START + 1)
                for k, (kind, c) in enumerate(FIN_FIRST):
                    evacuate(0, kind, c, k + 1)
                with act.Fori(0, N) as i:
                    for t in range(NT):
                        group, tile = TILES[t]
                        width = tile[1][3] + tile[1][2]
                        for h in range(2):
                            act.wait_ge(s_ready, START + 2 * NT * i + 2 * t + h + 1)
                            if h == 0:
                                ago, k = slot_user_before(t)
                                if ago == 0:
                                    act.wait_ge(pv_done, START + NT * i + k + 1)
                                if ago == 0 and k <= LAST_TILE[1]:
                                    act.wait_ge(added, START + POOL_OPS * i + pool_ops_before(k + 1))
                                if ago == 1:
                                    act.wait_ge(fin_written, START + fin_before(i, 0))
                                    act.wait_ge(added, START + POOL_OPS * i)
                            nc.scalar.activation(probs[h][:, t % NP_SLOTS, 0:width], ps_s[:, h, 0:width], ACT.Exp,
                                                 scale=SCORE_SCALE).then_inc(p_ready, 1)
                        for n in range(6 * t, 6 * t + 6 + (t == NT - 1)):
                            for u in range(NPROJ):
                                if PROJ_SLOT[u] == n:
                                    high(i + 1, u)
                            for k, (kind, c, at) in enumerate(FIN):
                                if at == n:
                                    if kind == "bc":
                                        masked_weight(i, c, fin_before(i, k) + 1)
                                    elif kind != "den":
                                        evacuate(values_pair(i, kind, c), kind, c, fin_before(i, k) + 1)

            @block.vector
            def _(dve):
                e = nc.vector

                def low(j, u):
                    c, m = divmod(u, 3)
                    if m == 2:
                        dve.wait_ge(proj_done, START + NPROJ * j + u + 1)
                        e.tensor_scalar(vt[:, cols(c)], ps_bg[:, u % 2, :], bias[:, 2:3], None,
                                        ALU.add).then_inc(proj_read, 1)
                        return
                    dve.wait_ge(hi_ready, START + 8 * j + 2 * c + m + 1)
                    e.scalar_tensor_tensor(lo[m][:, cols(c)], ps_bg[:, u % 2, :], bias[:, m:m + 1],
                                           hi[m][:, cols(c)].bitcast(F32), ALU.add, ALU.subtract
                                           ).then_inc(proj_read, 1)
                    if m == 0:
                        for h in range(2):
                            own = slice(64 * h, 64 * h + 64)
                            e.tensor_copy(q_pad[h][own, cols(c)], hi[0][own, cols(c)].bitcast(F32))
                    else:
                        e.tensor_copy(k_bf[:, cols(c)], hi[1][:, cols(c)].bitcast(F32)).then_inc(bf_ready, 1)

                def take_max(j, n):
                    h, qb, u, w = MAX_UNITS[n]
                    dve.wait_ge(max_scores, START + NMAX * j + n + 1)
                    if u == qb // 4:
                        e.memset(wait_here[:, n % 4:n % 4 + 1], 0.0)
                    to = partial[:, h, qb, u:u + 1]
                    if u == qb // 4:
                        e.tensor_tensor_reduce(junk[:, n % 2, 0:w], ps_bg[:, n % 2, 0:w], mask_q[:, CH - w:CH], 1.0,
                                               3 * NEVER, ALU.add, ALU.max, to).then_inc(max_read, 1)
                    else:
                        e.reduce_max(to, ps_bg[:, n % 2, 0:w], AX.X).then_inc(max_read, 1)
                    c = qb // 4
                    if n == LAST_MAX[c]:
                        dve.wait_ge(max_read, START + NMAX * j + n + 1)
                        e.tensor_reduce(neg_max[:, c, :].rearrange("p (h r) -> p h r", h=2),
                                        partial[:, :, 4 * c:4 * c + 4, :], AX.X, ALU.max,
                                        negate=True).then_inc(max_ready, 1)

                def scan(j, c):
                    e.tensor_tensor_scan(out=v_sum[:, cols(c)], data0=ones_row[:, :], data1=vt[:, cols(c)],
                                         initial=0.0, op0=ALU.mult, op1=ALU.add).then_inc(sums_ready, 1)
                    dve.wait_ge(sums_ready, START + 4 * j + (3 - c) + 1)
                    if c < 3:
                        dve.wait_ge(tail_ready, START + 4 * j + (3 - c))
                    e.tensor_tensor(v_tail[:, c:c + 1], v_tail[:, c + 1:c + 2], v_sum[:, CH * c + CH - 1:CH * c + CH],
                                    ALU.add).then_inc(tail_ready, 1)

                def masked_part(i, group, read):
                    dve.wait_ge(fin_read, START + read)
                    base = 3 * (4 * i + 3 - group)
                    dve.wait_ge(tail_ready, START + 4 * (i + 1))
                    e.tensor_scalar(e0[:, :], e0[:, :], 1.0, None, ALU.min).then_inc(step, 1)
                    dve.wait_ge(step, START + base + 1)
                    e.scalar_tensor_tensor(masked_num[:, :], v_sum[:, cols(group)], v_tail[:, group:group + 1],
                                           e0[:, :], ALU.subtract, ALU.mult).then_inc(step, 1)
                    e.scalar_tensor_tensor(masked_den[:, :], keys_after[:, :], float(CH * (3 - group)),
                                           e0[:, :], ALU.add, ALU.mult).then_inc(step, 1)

                def take_numerator(i, group):
                    dve.wait_ge(pv_done, START + NT * i + LAST_TILE[group] + 1)
                    dve.wait_ge(step, START + 3 * (4 * i + 3 - group) + 2)
                    dve.wait_ge(o_ready, START + 4 * i + 3 - group)
                    e.tensor_tensor(num[:, :], ps_o[:, :], masked_num[:, :], ALU.subtract).then_inc(num_ready, 1)

                def denominator(i, group, written):
                    n = 4 * i + 3 - group
                    dve.wait_ge(fin_written, START + written)
                    dve.wait_ge(step, START + 3 * n + 3)
                    e.tensor_tensor(den[:, :], ps_fin[:, :], masked_den[:, :], ALU.add).then_inc(fin_read, 1)

                def invert(i, group, quarter, written):
                    if quarter == 0:
                        dve.wait_ge(fin_read, START + written)
                    part = den[:, P * quarter:P * (quarter + 1)]
                    e.reciprocal(part, part).then_inc(counted, 1)

                def normalise(i, group):
                    n = 4 * i + 3 - group
                    dve.wait_ge(counted, START + 1 + 4 * (n + 1))
                    dve.wait_ge(num_ready, START + n + 1)
                    dve.wait_ge(o_stored[group % 2], START + 16 * (2 * i + (3 - group) // 2))
                    e.tensor_tensor(o_out[:, group % 2, :], num[:, :], den[:, :], ALU.mult).then_inc(o_ready, 1)

                e.memset(partial[:, :, :, 0:4], 3 * NEVER)
                e.memset(partial[:, :, :, 4:5], MASKED_RAW)
                e.memset(ones_row[:, :], 1.0).then_inc(counted, 1)
                for h in range(2):
                    e.memset(q_pad[h][:, :], 0.0)
                    e.memset(qm[h][64:128, :].bitcast(F32), 0.0)
                    e.memset(kl[h][64:128, :].bitcast(F32), 0.0)
                    e.memset(select[:, h, :].bitcast(F32), 0.0)
                e.memset(ones64[:, :], 1.0)
                e.memset(v_tail[:, :], 0.0)
                e.memset(masked_bias[:, :], MASKED)
                e.memset(neg_max[:, :, :], 0.0).then_inc(set_up, 1)
                dve.wait_ge(set_up, START + 1)
                for h in range(2):
                    e.memset(kl[h][64:65, :].bitcast(F32), 1.0)
                    e.memset(select[64:65, h, 64 * h:64 * h + 64].bitcast(F32), 1.0)
                dve.wait_ge(counted, START + 1)
                e.tensor_tensor_scan(out=num[:, :], data0=ones_row[:, :], data1=ones_row[:, :], initial=0.0,
                                     op0=ALU.mult, op1=ALU.add).then_inc(set_up, 1)
                dve.wait_ge(set_up, START + 2)
                dve.wait_ge(shaped, START + 6)
                e.tensor_scalar(keys_after[:, :], num[:, :], -1.0, float(CH), ALU.mult, ALU.add).then_inc(consts, 1)
                dve.wait_ge(consts, START + 1)

                dve.wait_ge(w_loaded, START + 144)
                for u in range(NPROJ):
                    low(0, u)
                for n in range(NMAX):
                    take_max(0, n)
                for c in (3, 2, 1):
                    scan(0, c)
                with dve.Fori(0, N) as i:
                    for n in range(SLOTS + 1):
                        for g in (3, 2, 1):
                            if n == 6 * (LAST_TILE[g] + 1):
                                take_numerator(i, g)
                        for u in range(NPROJ):
                            if PROJ_SLOT[u] == n:
                                low(i + 1, u)
                        if MAX_SLOT <= n < MAX_SLOT + NMAX:
                            take_max(i + 1, n - MAX_SLOT)
                        for k, (kind, c, at) in enumerate(FIN):
                            for quarter in range(4):
                                if kind == "den" and n == min(at + GAP * (quarter + 1), SLOTS):
                                    if quarter == 0 and at == n:
                                        take_numerator(i, 0)
                                        denominator(i, 0, fin_before(i, k) + 1)
                                    invert(i, c, quarter, fin_before(i, k) + 1)
                                    if quarter == 3:
                                        normalise(i, c)
                            if at == n:
                                if kind == "bc":
                                    masked_part(i, c, fin_before(i, k) + 1)
                                elif kind == "den" and at < SLOTS:
                                    denominator(i, c, fin_before(i, k) + 1)
                                elif kind == "vt":
                                    scan(values_pair(i, kind, c), c)


def feed_forward(nc, x, ot, wt, w_out, b_out, biases, gamma, beta, out):
    n_chunks = x.shape[0]
    D = w_out.shape[1]
    halves = D // P
    n_pairs = w_out.shape[0] // P
    n_blk = gamma.shape[0]
    with ExitStack() as ctx:
        def sb(name, shape, dt=F32):
            return ctx.enter_context(nc.sbuf_tensor(name, shape, dt))

        sems = []

        def sem(name):
            sems.append(ctx.enter_context(nc.semaphore(name)))
            return sems[-1]

        ident = sb("c_ident", [P, P])
        minus_half = sb("c_minus_half", [P, 4])
        wo = sb("c_wo", [P, n_pairs, D])
        w = sb("c_w", [P, 2 * n_blk, halves, D])
        b_out_row = sb("c_b_out_row", [P, D])
        b1_row = sb("c_b1_row", [P, n_blk, D])
        b2 = sb("c_b2", [P, n_blk, halves])
        ga = sb("c_ga", [P, n_blk, halves])
        be = sb("c_be", [P, n_blk, halves])
        o_in = [sb(f"c_o_in{L}", [P, n_pairs, CH]) for L in range(2)]
        x_in = [sb(f"c_x_in{L}", [P, 4, D]) for L in range(2)]
        xb = [sb(f"c_xb{L}", [P, 4, D]) for L in range(2)]
        x1 = [sb(f"c_x1{L}", [P, 4, D]) for L in range(2)]
        y = [sb(f"c_y{L}", [P, 4, D]) for L in range(2)]
        z = [sb(f"c_z{L}", [P, 4, D]) for L in range(2)]
        ht = [sb(f"c_ht{L}", [P, halves, CH]) for L in range(2)]
        yt = [sb(f"c_yt{L}", [P, halves, CH]) for L in range(2)]
        fin = [sb(f"c_fin{L}", [P, 4, D]) for L in range(2)]
        stats = [sb(f"c_stats{L}", [P, 4, 6]) for L in range(2)]
        mv = [sb(f"c_mv{L}", [P, 4, 2]) for L in range(2)]
        var_eps = [sb(f"c_var{L}", [P, 4]) for L in range(2)]
        rstd = [sb(f"c_rstd{L}", [P, 4]) for L in range(2)]
        ps_y = [ctx.enter_context(nc.psum_tensor(f"c_ps_y{L}", [P, 4, D], F32)) for L in range(2)]
        ps_t = [ctx.enter_context(nc.psum_tensor(f"c_ps_t{L}", [P, halves, CH], F32)) for L in range(2)]

        wait_here = sb("c_wait_here", [P, 1])

        zeroed = sem("c_zeroed")
        ident_ready = sem("c_ident_ready")
        w_loaded = sem("c_w_loaded")
        o_loaded = [sem(f"c_o_loaded{L}") for L in range(2)]
        x_loaded = [sem(f"c_x_loaded{L}") for L in range(2)]
        xb_ready = [sem(f"c_xb_ready{L}") for L in range(2)]
        y_summed = [sem(f"c_y_summed{L}") for L in range(2)]
        y_taken = [sem(f"c_y_taken{L}") for L in range(2)]
        stats_done = [sem(f"c_stats_done{L}") for L in range(2)]
        mv_done = [sem(f"c_mv_done{L}") for L in range(2)]
        var_done = [sem(f"c_var_done{L}") for L in range(2)]
        rstd_done = [sem(f"c_rstd_done{L}") for L in range(2)]
        z_ready = [sem(f"c_z_ready{L}") for L in range(2)]
        z_turned = [sem(f"c_z_turned{L}") for L in range(2)]
        t_taken = [sem(f"c_t_taken{L}") for L in range(2)]
        h_summed = [sem(f"c_h_summed{L}") for L in range(2)]
        h_ready = [sem(f"c_h_ready{L}") for L in range(2)]
        stored = [sem(f"c_stored{L}") for L in range(2)]

        YS = 2 + n_blk
        ZS = 1 + n_blk

        loads = [(wo[:, :, :], w_out.rearrange("(a p) d -> p a d", p=P)),
                 (b_out_row[:, :], b_out.rearrange("(o d) -> o d", o=1).to_broadcast([P, D]))]
        for l in range(2 * n_blk):
            loads.append((w[:, l], wt[l]))
        for k in range(n_blk):
            loads.append((b1_row[:, k, :], biases[2 * k:2 * k + 1, :].to_broadcast([P, D])))
            for s in range(halves):
                half = slice(s * P, (s + 1) * P)
                loads.append((b2[:, k, s:s + 1], biases[2 * k + 1:2 * k + 2, half].rearrange("o p -> p o")))
                loads.append((ga[:, k, s:s + 1], gamma[k:k + 1, half].rearrange("o p -> p o")))
                loads.append((be[:, k, s:s + 1], beta[k:k + 1, half].rearrange("o p -> p o")))

        start_counts(nc, sems)
        with nc.Block() as block:
            @block.sync
            def _(sp):
                for dst, src in loads:
                    sp.dma_start(dst, src).then_inc(w_loaded, 16)

                def load(i, L):
                    g = (2 * i + L) % n_chunks
                    sp.dma_start(o_in[L][:, :, :], ot.rearrange("b a c p t -> b c p a t")[g // 4, 3 - g % 4]
                                 ).then_inc(o_loaded[L], 16)
                    sp.dma_start(x_in[L][:, :, :], x[g]).then_inc(x_loaded[L], 16)

                for L in range(2):
                    load(0, L)
                with sp.Fori(0, n_chunks // 2) as i:
                    for L in range(2):
                        sp.wait_ge(xb_ready[L], START + i + 1)
                        sp.wait_ge(y_summed[L], START + YS * i + 1)
                        load(i + 1, L)
                    for L in range(2):
                        sp.wait_ge(y_taken[L], START + YS * i + YS)
                        sp.dma_start(out[2 * i + L], fin[L][:, :, :]).then_inc(stored[L], 16)
                for L in range(2):
                    sp.wait_ge(stored[L], START + 16 * (n_chunks // 2))
                    sp.wait_ge(o_loaded[L], START + 16 * (n_chunks // 2 + 1))
                    sp.wait_ge(x_loaded[L], START + 16 * (n_chunks // 2 + 1))

            @block.gpsimd
            def _(pool):
                nc.gpsimd.memset(ident[:, :], 0.0).then_inc(zeroed, 1)
                nc.gpsimd.memset(minus_half[:, :], -0.5).then_inc(zeroed, 1)
                pool.wait_ge(zeroed, START + 2)
                nc.gpsimd.affine_select(out=ident[:, :], in_=ident[:, :], compare_op=ALU.not_equal, fill=1.0,
                                        base=0, pattern=[[-1, P]], channel_multiplier=1).then_inc(ident_ready, 1)
                pool.wait_ge(w_loaded, START + 16 * len(loads))
                with pool.Fori(0, n_chunks // 2) as i:
                    for L in range(2):
                        pool.wait_ge(x_loaded[L], START + 16 * i + 16)
                        pool.wait_ge(y_taken[L], START + YS * i)
                        nc.gpsimd.tensor_tensor(xb[L][:, :, :], x_in[L][:, :, :],
                                                b_out_row[:, :].unsqueeze(1).to_broadcast([P, 4, D]),
                                                ALU.add).then_inc(xb_ready[L], 1)
                    for k in range(ZS):
                        for L in range(2):
                            pool.wait_ge(var_done[L], START + ZS * i + k + 1)
                            nc.gpsimd.tensor_tensor(rstd[L][:, :], var_eps[L][:, :], minus_half[:, :],
                                                    ALU.pow).then_inc(rstd_done[L], 1)

            @block.tensor
            def _(pe):
                pe.wait_ge(ident_ready, START + 1)
                pe.wait_ge(w_loaded, START + 16 * len(loads))

                def turn_z(i, k, L):
                    pe.wait_ge(z_ready[L], START + ZS * i + k + 1)
                    pe.wait_ge(h_ready[L], START + n_blk * i + max(k - 1, 0))
                    for s in range(halves):
                        for t in range(4):
                            mm = pe.transpose(ps_t[L][:, s, t * P:(t + 1) * P], z[L][:, t, s * P:(s + 1) * P],
                                              ident[:, :])
                    mm.then_inc(z_turned[L], 1)

                with pe.Fori(0, n_chunks // 2) as i:
                    for L in range(2):
                        pe.wait_ge(o_loaded[L], START + 16 * i + 16)
                        pe.wait_ge(y_taken[L], START + YS * i)
                        for t in range(4):
                            for a in range(n_pairs):
                                mm = pe.matmul(ps_y[L][:, t, :], o_in[L][:, a, t * P:(t + 1) * P], wo[:, a, :],
                                               start=(a == 0 and t % 2 == 0), stop=(a == n_pairs - 1),
                                               skip_group_check=True)
                        mm.then_inc(y_summed[L], 1)
                    for L in range(2):
                        turn_z(i, 0, L)
                    for k in range(n_blk):
                        for L in range(2):
                            if k == 0:
                                pe.wait_ge(t_taken[L], START + ZS * i + 1)
                            else:
                                pe.wait_ge(h_ready[L], START + n_blk * i + k)
                            pe.wait_ge(y_taken[L], START + YS * i + 1 + k)
                            for t in range(4):
                                for s in range(halves):
                                    mm = pe.matmul(ps_y[L][:, t, :], ht[L][:, s, t * P:(t + 1) * P], w[:, 2 * k, s, :],
                                                   start=(s == 0 and t % 2 == 0), stop=(s == halves - 1),
                                                   skip_group_check=True)
                            mm.then_inc(y_summed[L], 1)
                        for L in range(2):
                            turn_z(i, k + 1, L)
                        for L in range(2):
                            pe.wait_ge(t_taken[L], START + ZS * i + k + 2)
                            for s in range(halves):
                                for r in range(halves):
                                    mm = pe.matmul(ps_t[L][:, s, :], w[:, 2 * k + 1, r, s * P:(s + 1) * P], yt[L][:, r, :],
                                                   start=(r == 0), stop=(r == halves - 1))
                            mm.then_inc(h_summed[L], 1)
                    for L in range(2):
                        pe.wait_ge(h_ready[L], START + n_blk * i + n_blk)
                        for t in range(4):
                            for s in range(halves):
                                mm = pe.transpose(ps_y[L][:, t, s * P:(s + 1) * P], ht[L][:, s, t * P:(t + 1) * P],
                                                  ident[:, :])
                        mm.then_inc(y_summed[L], 1)

            @block.scalar
            def _(act):
                act.wait_ge(w_loaded, START + 16 * len(loads))
                with act.Fori(0, n_chunks // 2) as i:
                    for L in range(2):
                        act.wait_ge(z_turned[L], START + ZS * i + 1)
                        act.wait_ge(y_summed[L], START + YS * i)
                        nc.scalar.copy(ht[L][:, :, :], ps_t[L][:, :, :]).then_inc(t_taken[L], 1)
                    for k in range(n_blk):
                        for L in range(2):
                            act.wait_ge(z_turned[L], START + ZS * i + k + 2)
                            act.wait_ge(h_summed[L], START + n_blk * i + k)
                            for s in range(halves):
                                a = nc.scalar.activation(yt[L][:, s, :], ps_t[L][:, s, :], ACT.Gelu,
                                                         bias=be[:, k, s:s + 1], scale=ga[:, k, s:s + 1])
                            a.then_inc(t_taken[L], 1)

            @block.vector
            def _(dve):
                e = nc.vector
                dve.wait_ge(w_loaded, START + 16 * len(loads))

                def normalised(i, k, L, src):
                    n = ZS * i + k
                    dve.wait_ge(y_taken[L], START + YS * i + k + 1)
                    for t in range(4):
                        e.bn_stats(stats[L][:, t, :], src[:, t, :]).then_inc(stats_done[L], 1)
                    dve.wait_ge(stats_done[L], START + 4 * n + 4)
                    e.memset(wait_here[:, :], 0.0)
                    for t in range(4):
                        e.bn_aggr(mv[L][:, t, :], stats[L][:, t, :]).then_inc(mv_done[L], 1)
                    dve.wait_ge(mv_done[L], START + 4 * n + 4)
                    e.tensor_scalar(var_eps[L][:, :], mv[L][:, :, 1], LN_EPS, None, ALU.add).then_inc(var_done[L], 1)

                def scaled(i, k, L, src):
                    n = ZS * i + k
                    dve.wait_ge(rstd_done[L], START + n + 1)
                    dve.wait_ge(z_turned[L], START + n)
                    for t in range(4):
                        a = e.tensor_scalar(z[L][:, t, :], src[:, t, :], mv[L][:, t, 0:1], rstd[L][:, t:t + 1],
                                            ALU.subtract, ALU.mult)
                    a.then_inc(z_ready[L], 1)

                with dve.Fori(0, n_chunks // 2) as i:
                    for L in range(2):
                        dve.wait_ge(y_summed[L], START + YS * i + 1)
                        dve.wait_ge(xb_ready[L], START + i + 1)
                        e.tensor_tensor(x1[L][:, :, :], ps_y[L][:, :, :], xb[L][:, :, :], ALU.add).then_inc(y_taken[L], 1)
                        normalised(i, 0, L, x1[L])
                    for L in range(2):
                        scaled(i, 0, L, x1[L])
                    for k in range(n_blk):
                        for L in range(2):
                            dve.wait_ge(y_summed[L], START + YS * i + 2 + k)
                            e.tensor_tensor(y[L][:, :, :], ps_y[L][:, :, :],
                                            b1_row[:, k, :].unsqueeze(1).to_broadcast([P, 4, D]),
                                            ALU.add).then_inc(y_taken[L], 1)
                            normalised(i, k + 1, L, y[L])
                        for L in range(2):
                            scaled(i, k + 1, L, y[L])
                        for L in range(2):
                            dve.wait_ge(h_summed[L], START + n_blk * i + k + 1)
                            for s in range(halves):
                                a = e.scalar_tensor_tensor(ht[L][:, s, :], ps_t[L][:, s, :], b2[:, k, s:s + 1],
                                                           ht[L][:, s, :], ALU.add, ALU.add)
                            a.then_inc(h_ready[L], 1)
                    for L in range(2):
                        dve.wait_ge(y_summed[L], START + YS * i + YS)
                        dve.wait_ge(stored[L], START + 16 * i)
                        e.tensor_tensor(fin[L][:, :, :], ps_y[L][:, :, :], x1[L][:, :, :], ALU.add
                                        ).then_inc(y_taken[L], 1)


def program(nc, residual, w_key, w_query, w_values, w_output, b_key, b_query, b_values, b_output,
            qweights, scales, biases, lora_a, lora_b, ln_gamma, ln_beta, out):
    B, S, D = residual.shape
    n_heads, _, H = w_key.shape
    n_chunks = B * S // CH
    halves = D // P
    n_pairs = n_heads // 2
    xnt = nc.dram_tensor("xn_turned", [n_chunks, P, halves, CH], F32).ap()
    wt = nc.dram_tensor("weights_turned", [qweights.shape[0], P, halves, D], F32).ap()
    ot = nc.dram_tensor("heads_turned", [B, n_pairs, 4, P, CH], F32).ap()
    x = residual.rearrange("b (c t p) d -> (b c) p t d", c=S // CH, p=P)
    y = out.rearrange("b (c t p) d -> (b c) p t d", c=S // CH, p=P)
    layernorm_and_weights(nc, x, qweights, scales, lora_a, lora_b, xnt, wt)
    attention(nc, xnt, [w_query, w_key, w_values], [b_query, b_key, b_values], ot)
    feed_forward(nc, x, ot, wt, w_output.rearrange("n h e -> (n h) e"), b_output, biases, ln_gamma, ln_beta, y)


_INS = ["L0_attn_residual", "L0_attn_W_key", "L0_attn_W_query", "L0_attn_W_values", "L0_attn_W_output",
        "L0_attn_Bias_key", "L0_attn_Bias_query", "L0_attn_Bias_values", "L0_attn_Bias_output",
        "L0_ffn_qweights", "L0_ffn_scales", "L0_ffn_biases", "L0_ffn_lora_a", "L0_ffn_lora_b",
        "L0_ffn_ln_gamma", "L0_ffn_ln_beta"]


def kernel(**inputs):
    import concourse.bacc as bacc
    from concourse.bass_utils import run_bass_kernel_spmd as run

    nc = bacc.Bacc("TRN2", target_bir_lowering=False, num_devices=1)
    arrays, args = {}, []
    for name in _INS:
        a = np.ascontiguousarray(inputs[name])
        arrays[f"in_{name}"] = a
        args.append(nc.dram_tensor(f"in_{name}", a.shape, mybir.dt.from_np(a.dtype), kind="ExternalInput").ap())
    shape = arrays["in_L0_attn_residual"].shape
    args.append(nc.dram_tensor("out_0", shape, F32, kind="ExternalOutput").ap())
    program(nc, *args)
    r = run(nc, [arrays], core_ids=[0])
    return r.results[0]["out_0"]
```
